# Optimizing a Trainium2 kernel written in Bass

```python
import numpy as np
import jax
import jax.numpy as jnp

def _softmax(x, axis=-1):
    return jax.nn.softmax(x, axis=axis)

def _gelu(x):
    return jax.nn.gelu(x, approximate=True)

def _silu(x):
    return jax.nn.silu(x)

def _sigmoid(x):
    return jax.nn.sigmoid(x)

def _layernorm(x, axis=-1, eps=1e-05):
    m = jnp.mean(x, axis=axis, keepdims=True)
    v = jnp.var(x, axis=axis, keepdims=True)
    return (x - m) / jnp.sqrt(v + eps)

def _scatter_add(tgt, idx, src, axis=0):
    return tgt.at[idx].add(src)

def _segment_sum(src, seg, n):
    return jax.ops.segment_sum(src, seg, n)
kernel_name = 'mk_gnn_preln_d2_gnn_r8_b32c88'

def setup_inputs(seed: int=0):
    np.random.seed(seed)
    _w = jnp.asarray

    def _rec_inputs():
        import jax
        import jax.numpy as jnp
        _gk = jax.random.key(seed)
        x = -0.0001006 + 1 * jax.random.normal(jax.random.fold_in(_gk, 1), (12500, 96), jnp.float32)
        src = jax.random.randint(jax.random.fold_in(_gk, 2), (400000,), 0, 12500, jnp.int32)
        dst = jnp.minimum((12500 * jax.random.uniform(jax.random.fold_in(_gk, 3), (400000,)) ** 2.0).astype(jnp.int32), 99999)
        _o = jnp.argsort(dst, stable=True)
        src = src[_o]
        dst = dst[_o]
        edge_attr_32 = 0.000196303 + 1.00016 * jax.random.normal(jax.random.fold_in(_gk, 11), (400000, 32), jnp.float32)
        return (x, src, dst, edge_attr_32)
    x, src, dst, edge_attr_32 = _rec_inputs()

    def _L0_gnn_setup():
        import jax, jax.numpy as jnp
        import numpy as np
        BN_EPS = 1e-05
        key = jax.random.key(seed)
        ks = jax.random.split(key, 5)
        N, E, D = (6250, 100000, 96)
        x = jax.random.normal(ks[0], (N, D), dtype=jnp.float32)
        edge_index = jax.random.randint(ks[1], (2, E), 0, N, dtype=jnp.int64)
        Wl = jax.random.normal(ks[2], (D, D), dtype=jnp.float32) / np.sqrt(D)
        bl = jnp.zeros((D,), dtype=jnp.float32)
        Wr = jax.random.normal(ks[3], (D, D), dtype=jnp.float32) / np.sqrt(D)
        gamma = jnp.ones((D,), dtype=jnp.float32)
        beta = jnp.zeros((D,), dtype=jnp.float32)
        return {'x': x, 'edge_index': edge_index, 'Wl': Wl, 'bl': bl, 'Wr': Wr, 'gamma': gamma, 'beta': beta}
    _L0_gnn_all = _L0_gnn_setup()
    _L0_gnn_in = {k: v for k, v in _L0_gnn_all.items() if k in ('Wl', 'bl', 'Wr', 'gamma', 'beta')}
    del _L0_gnn_all

    def _L1_gnn_setup():
        import jax, jax.numpy as jnp
        import numpy as np
        N, E = (6250, 100000)
        DIN = DOUT = 96
        DE = 32

        def _egnn_conv(x, src, dst, edge_attr, W_msg, W_edge, W_root, b):
            msg = x[src] @ W_msg + edge_attr @ W_edge
            agg = jax.ops.segment_max(msg, dst, num_segments=x.shape[0])
            agg = jnp.where(jnp.isneginf(agg), 0.0, agg)
            return agg + x @ W_root + b
        key = jax.random.key(seed)
        ks = jax.random.split(key, 10)
        rn = lambda k, sh, sc: jax.random.normal(k, sh, jnp.float32) * sc
        return {'X': rn(ks[0], (N, DIN), 1.0), 'edge_index': jax.random.randint(ks[1], (2, E), 0, N, jnp.int32), 'edge_attr': rn(ks[2], (E, DE), 1.0), 'W1_msg': rn(ks[3], (DIN, DOUT), DIN ** (-0.5)), 'W1_edge': rn(ks[4], (DE, DOUT), DE ** (-0.5)), 'W1_root': rn(ks[5], (DIN, DOUT), DIN ** (-0.5)), 'b1': jnp.zeros((DOUT,), jnp.float32), 'W2_msg': rn(ks[6], (DOUT, DOUT), DOUT ** (-0.5)), 'W2_edge': rn(ks[7], (DE, DOUT), DE ** (-0.5)), 'W2_root': rn(ks[8], (DOUT, DOUT), DOUT ** (-0.5)), 'b2': jnp.zeros((DOUT,), jnp.float32)}
    _L1_gnn_all = _L1_gnn_setup()
    _L1_gnn_in = {k: v for k, v in _L1_gnn_all.items() if k in ('W1_msg', 'W1_edge', 'W1_root', 'b1', 'W2_msg', 'W2_edge', 'W2_root', 'b2')}
    del _L1_gnn_all
    return {'x': x, 'src': src, 'dst': dst, 'edge_attr_32': edge_attr_32, 'L0_gnn_Wl': _L0_gnn_in['Wl'], 'L0_gnn_bl': _L0_gnn_in['bl'], 'L0_gnn_Wr': _L0_gnn_in['Wr'], 'L0_gnn_gamma': _L0_gnn_in['gamma'], 'L0_gnn_beta': _L0_gnn_in['beta'], 'L1_gnn_W1_msg': _L1_gnn_in['W1_msg'], 'L1_gnn_W1_edge': _L1_gnn_in['W1_edge'], 'L1_gnn_W1_root': _L1_gnn_in['W1_root'], 'L1_gnn_b1': _L1_gnn_in['b1'], 'L1_gnn_W2_msg': _L1_gnn_in['W2_msg'], 'L1_gnn_W2_edge': _L1_gnn_in['W2_edge'], 'L1_gnn_W2_root': _L1_gnn_in['W2_root'], 'L1_gnn_b2': _L1_gnn_in['b2']}

def reference(x, src, dst, edge_attr_32, L0_gnn_Wl, L0_gnn_bl, L0_gnn_Wr, L0_gnn_gamma, L0_gnn_beta, L1_gnn_W1_msg, L1_gnn_W1_edge, L1_gnn_W1_root, L1_gnn_b1, L1_gnn_W2_msg, L1_gnn_W2_edge, L1_gnn_W2_root, L1_gnn_b2):
    import jax
    import jax.numpy as jnp

    def _L0_gnn_ref(x, edge_index, Wl, bl, Wr, gamma, beta):
        import jax, jax.numpy as jnp
        import numpy as np
        BN_EPS = 1e-05
        N = x.shape[0]
        src, dst = (edge_index[0], edge_index[1])
        msg_sum = jax.ops.segment_sum(x[src], dst, num_segments=N)
        deg = jax.ops.segment_sum(jnp.ones_like(src, dtype=x.dtype), dst, num_segments=N)
        neigh_mean = msg_sum / jnp.maximum(deg, 1.0)[:, None]
        h = jnp.einsum('nd,od->no', neigh_mean, Wl) + bl + jnp.einsum('nd,od->no', x, Wr)
        mu = h.mean(axis=0)
        var = h.var(axis=0)
        h = (h - mu) * jax.lax.rsqrt(var + BN_EPS) * gamma + beta
        return jax.nn.relu(h)

    def _L1_gnn_ref(X, edge_index, edge_attr, W1_msg, W1_edge, W1_root, b1, W2_msg, W2_edge, W2_root, b2):
        import jax, jax.numpy as jnp
        import numpy as np
        N, E = (6250, 100000)
        DIN = DOUT = 96
        DE = 32

        def _egnn_conv(x, src, dst, edge_attr, W_msg, W_edge, W_root, b):
            msg = x[src] @ W_msg + edge_attr @ W_edge
            agg = jax.ops.segment_max(msg, dst, num_segments=x.shape[0])
            agg = jnp.where(jnp.isneginf(agg), 0.0, agg)
            return agg + x @ W_root + b
        src, dst = (edge_index[0], edge_index[1])
        c1 = jax.nn.leaky_relu(_egnn_conv(X, src, dst, edge_attr, W1_msg, W1_edge, W1_root, b1))
        c2 = jax.nn.leaky_relu(_egnn_conv(c1, src, dst, edge_attr, W2_msg, W2_edge, W2_root, b2))
        return c2
    edge_index = jnp.stack([src, dst])
    h = jnp.maximum(_layernorm(x, axis=-1), 0.0)
    x = x + _L0_gnn_ref(h, edge_index, L0_gnn_Wl, L0_gnn_bl, L0_gnn_Wr, L0_gnn_gamma, L0_gnn_beta)
    h = jnp.maximum(_layernorm(x, axis=-1), 0.0)
    x = x + _L1_gnn_ref(h, edge_index, edge_attr_32, L1_gnn_W1_msg, L1_gnn_W1_edge, L1_gnn_W1_root, L1_gnn_b1, L1_gnn_W2_msg, L1_gnn_W2_edge, L1_gnn_W2_root, L1_gnn_b2)
    return x

_drawn_inputs = setup_inputs


def setup_inputs(seed=0):
    import zlib

    import numpy as np

    out = dict(_drawn_inputs(seed))
    spreads = {'L0_gnn_bl': (0.0, 0.8),
     'L0_gnn_gamma': (1.0, 0.2),
     'L0_gnn_beta': (0.0, 0.354),
     'L1_gnn_b1': (0.0, 0.35),
     'L1_gnn_b2': (0.0, 0.354)}
    factors = {}
    for name, (base, spread) in spreads.items():
        noise = np.random.default_rng([zlib.crc32(name.encode()), seed]).standard_normal(out[name].shape)
        drawn = base * np.exp(spread * noise) if base else spread * noise
        out[name] = jnp.asarray(drawn.astype(out[name].dtype))
    for name, factor in factors.items():
        out[name] = (out[name] * factor).astype(out[name].dtype)
    return out
```

```python
import concourse.bass as bass
from concourse import mybir
from contextlib import ExitStack

F32 = mybir.dt.float32
BF16 = mybir.dt.bfloat16
I32 = mybir.dt.int32
ALU = mybir.AluOpType
ACT = mybir.ActivationFunctionType

N, D, E, DE = 12500, 96, 400000, 32
P = 128
EP = E // P
NP = 125
TILES = N // NP
GT = 4
GROUPS = TILES // GT
GCOLS = GT * NP
GBODY = 4
GLOOPS = GROUPS // GBODY
U = 24
CLOOPS = EP // (2 * U)
LASTU = EP - 2 * U * CLOOPS
QG = U // 4
LASTCOL = EP - LASTU
BIG = 3.0e38
NOWHERE = float(1 << 23)
NWIDE = 112
EPS = 1e-5
SLOPE = 0.01
N_W = 19

assert GROUPS == GBODY * GLOOPS + 1 and NP * TILES == N and EP * P == E and LASTU == 5


def gnn_kernel(nc, x, src, dst, ea_main, ea_tail, ea_last, wlT, bl, wrT, gamma, beta,
               w1_msg, w1_edge, w1_root, b1, w2_msg, w2_edge, w2_root, b2, out):
    ctx = ExitStack()
    with ctx:
        def sb(name, shape, dt=F32):
            return ctx.enter_context(nc.sbuf_tensor(name, shape, dt))

        def sem(name):
            return ctx.enter_context(nc.semaphore(name))

        table = nc.dram_tensor("table", (N, D), F32, kind="Internal").ap()
        states = nc.dram_tensor("states", (E, D), F32, kind="Internal").ap()
        last_dram = nc.dram_tensor("last_dram", (N, 1), F32, kind="Internal").ap()
        x_v = x.rearrange("(p t) d -> p t d", p=NP)
        out_v = out.rearrange("(p t) d -> p t d", p=NP)
        table_v = table.rearrange("(p t) d -> p t d", p=NP)
        states_v = states.rearrange("(p j) d -> p j d", p=P)
        last_v = last_dram.rearrange("(p t) a -> p (t a)", p=NP)
        src_v = src.rearrange("(p j) -> p j", p=P)
        dst_v = dst.rearrange("(p j) -> p j", p=P)

        X = sb("X", [NP, TILES, D])
        R = sb("R", [NP, TILES, D])
        FT = sb("FT", [P, GROUPS * GCOLS])
        ROOT = FT[0:NP, 0:TILES * D].rearrange("p (t d) -> p t d", t=TILES)
        same = sb("same", [P, EP])
        gbuf = [sb(f"gbuf{b}", [P, U, D]) for b in range(2)]
        idx = [sb(f"idx{b}", [P, U], I32) for b in range(2)]
        mask = [sb(f"mask{b}", [P, U]) for b in range(2)]
        ea = [sb(f"ea{b}", [P, QG, P]) for b in range(2)]
        carry = sb("carry", [P, D])
        lidx = [sb(f"lidx{s}", [NP, GT], I32) for s in range(GBODY)]
        nodeA = [sb(f"nodeA{k}", [NP, GT, D]) for k in range(2)]
        featA = [sb(f"featA{k}", [D + 1, GCOLS]) for k in range(2)]
        nodeB = [sb(f"nodeB{k}", [NP, GT, D]) for k in range(2)]
        featB = [sb(f"featB{k}", [D, GCOLS]) for k in range(2)]
        ft16 = FT[:, :].bitcast(BF16)
        hi = ft16[:, 0:EP]
        lo = ft16[:, EP:2 * EP]
        OHW = NP + TILES
        oh = [ft16[:, 2 * EP + b * U * OHW:2 * EP + (b + 1) * U * OHW] for b in range(2)]
        oh_hi = [o[:, 0:U * NP].rearrange("p (u w) -> p u w", u=U) for o in oh]
        oh_lo = [o[:, U * NP:U * OHW].rearrange("p (u w) -> p u w", u=U) for o in oh]
        assert 4 * EP == GROUPS * GCOLS
        dst_f = FT[:, EP:2 * EP]
        dst_i = FT[:, 2 * EP:3 * EP].bitcast(I32)
        quot_f = FT[:, 2 * EP:3 * EP]
        quot_i = FT[:, 3 * EP:4 * EP].bitcast(I32)
        rest_f = FT[:, 3 * EP:4 * EP]
        ident = sb("ident", [P, P])
        ones = sb("ones", [P, P])
        below = sb("below", [P, P])
        ramp_i = sb("ramp_i", [P, P], I32)
        ramp = sb("ramp", [P, P], BF16)
        zero16 = sb("zero16", [P, P], BF16)
        stats = sb("stats", [NP, TILES, 6])
        ln_a = sb("ln_a", [NP, TILES])
        ln_b = sb("ln_b", [NP, TILES])
        ln_c = sb("ln_c", [NP, TILES])
        ln_d = sb("ln_d", [NP, TILES])
        rstd = sb("rstd", [NP, TILES])
        shift = sb("shift", [NP, TILES])
        eps = sb("eps", [P, 1])
        hist = sb("hist", [NP, TILES])
        upto = sb("upto", [NP, TILES])
        last_f = sb("last_f", [NP, TILES])
        last_i = sb("last_i", [NP, GT * (GROUPS + GBODY)], I32)
        inv_deg = sb("inv_deg", [NP, TILES])
        empty = sb("empty", [NP, TILES])
        prefix = sb("prefix", [NP, 1])
        first_i = sb("first_i", [P, 1], I32)
        first_f = sb("first_f", [P, 1])
        lastd_f = sb("lastd_f", [P, 1])
        prev_i = sb("prev_i", [P, 1], I32)
        prev_f = sb("prev_f", [P, 1])
        joins = sb("joins", [P, 1])
        spans = sb("spans", [P, 1])
        chain_end_i = sb("chain_end_i", [P, 1], I32)
        chain_end = sb("chain_end", [P, 1])
        first_last = sb("first_last", [P, 1])
        fix_ok = sb("fix_ok", [P, 1])
        fix_f = sb("fix_f", [P, 1])
        fix_i = sb("fix_i", [P, 1], I32)
        diag = sb("diag", [P, P])
        span_mul = sb("span_mul", [D, P])
        span_add = sb("span_add", [D, P])
        chainT = sb("chainT", [D, P + 1])
        fix_rows = sb("fix_rows", [P, D])
        bstats = sb("bstats", [D, GROUPS, 6])
        bmv = sb("bmv", [D, 2])
        bstd = sb("bstd", [D, 1])
        bscale = sb("bscale", [D, 1])
        bshift = sb("bshift", [D, 1])
        Wl = sb("Wl", [D, D])
        Wr = sb("Wr", [D, D])
        Wmo = [None] + [sb(f"Wmo{k}", [D + 1, 2 * D]) for k in (1, 2)]
        We = [None, sb("We1", [P, 4 * D]), sb("We2", [P, 4 * D])]
        cols = sb("cols", [D, 3])

        psum = ctx.enter_context(nc.psum_tensor("psum", [P, 8 * 512], F32))
        bank = [psum[:, n * 512:(n + 1) * 512] for n in range(8)]
        HIST = bank[7][0:NP, 0:TILES]

        s_x = [sem(f"s_xblock{n}") for n in range(5)]
        s_dst = sem("s_dst")
        s_edge = sem("s_edge")
        s_w = sem("s_w")
        s_clear = sem("s_clear")
        s_const = sem("s_const")
        s_v = sem("s_v")
        s_same = sem("s_same")
        s_bnsraw = sem("s_bnsraw")
        s_var = sem("s_var")
        s_std = sem("s_std")
        s_norm = sem("s_norm")
        s_h0 = sem("s_h0")
        s_tab = [sem(f"s_tab{k}") for k in range(3)]
        s_idx = [[sem(f"s_idx{k}{b}") for b in range(2)] for k in range(3)]
        s_gath = [[sem(f"s_gath{k}{b}") for b in range(2)] for k in range(3)]
        s_wrote = [[sem(f"s_wrote{k}{b}") for b in range(2)] for k in range(3)]
        s_mask = [sem(f"s_mask{k}") for k in range(3)]
        s_chain = [sem(f"s_chain{k}") for k in range(3)]
        s_ea = [None] + [[sem(f"s_ea{k}{b}") for b in range(2)] for k in (1, 2)]
        s_q = [None] + [sem(f"s_q{k}") for k in (1, 2)]
        s_qadd = [None] + [sem(f"s_qadd{k}") for k in (1, 2)]
        s_oh = sem("s_oh")
        s_ohmul = sem("s_ohmul")
        s_hist0 = sem("s_hist0")
        s_hist = sem("s_hist")
        s_upto = sem("s_upto")
        s_prefix = sem("s_prefix")
        s_lastf = sem("s_lastf")
        s_lastd = sem("s_lastd")
        s_flast = sem("s_flast")
        s_fixi = sem("s_fixi")
        s_diag = sem("s_diag")
        s_span = sem("s_span")
        s_go = sem("s_go")
        s_tail = [sem(f"s_tail{k}") for k in range(3)]
        s_scan = [sem(f"s_scan{k}") for k in range(3)]
        s_back = [sem(f"s_back{k}") for k in range(3)]
        s_fixz = [sem(f"s_fixz{k}") for k in range(3)]
        s_fixg = [sem(f"s_fixg{k}") for k in range(3)]
        s_fixed = [sem(f"s_fixed{k}") for k in range(3)]
        s_fixw = [sem(f"s_fixw{k}") for k in range(3)]
        s_slot = [sem(f"s_slot{k}") for k in range(3)]
        s_ext = [[sem(f"s_ext{k}{s}") for s in range(GBODY)] for k in range(3)]
        s_mean = sem("s_mean")
        s_tA = [sem(f"s_tA{k}") for k in range(3)]
        s_eA = [sem(f"s_eA{k}") for k in range(3)]
        s_tB = sem("s_tB")
        s_eB = sem("s_eB")
        s_mm = sem("s_mm")
        s_ft = sem("s_ft")
        s_bst = sem("s_bst")
        s_bvar = sem("s_bvar")
        s_bstd = sem("s_bstd")
        s_bn = sem("s_bn")
        s_y = sem("s_y")
        s_yT = sem("s_yT")
        s_x1 = sem("s_x1")
        s_h1 = sem("s_h1")
        s_c = sem("s_c")
        s_pm = [None] + [sem(f"s_pm{k}") for k in (1, 2)]
        s_pe = [None] + [sem(f"s_pe{k}") for k in (1, 2)]
        s_re = [None] + [sem(f"s_re{k}") for k in (1, 2)]
        s_nB = sem("s_nB")
        s_c2 = sem("s_c2")
        s_out = sem("s_out")

        STEPS = U + 1
        CHAIN_ALL = STEPS * 2 * CLOOPS + LASTU + 1
        XT = TILES // 5
        TABLE_DONE = [32 * 5] + [32 * (GLOOPS + 1)] * 2
        LASTQ = 2

        def groups(eng, body):
            with eng.Fori(0, GLOOPS) as i:
                for s in range(GBODY):
                    body(i * GBODY + s, s, i)
            body(GROUPS - 1, 0, GLOOPS)

        def chunks(eng, body):
            with eng.Fori(0, CLOOPS) as i:
                for b in range(2):
                    body(i * 2 + b, i, b, U, i * (2 * U) + b * U)
            body(2 * CLOOPS, CLOOPS, 0, LASTU, LASTCOL)

        def node_dma(eng, to, of, done):
            eng.dma_start(to[0:NWIDE], of[0:NWIDE]).then_inc(done, 16)
            eng.dma_start(to[NWIDE:NP], of[NWIDE:NP]).then_inc(done, 16)

        def group_of(t, g):
            return t[:, bass.ds(g * GT, GT), :]

        def ft_of(g):
            return FT[0:D, bass.ds(g * GCOLS, GCOLS)]

        def wide(b, cols=GCOLS):
            return bank[b][0:D, 0:cols]

        def narrow(b):
            return bank[b][0:NP, 0:GT * D].rearrange("p (t d) -> p t d", t=GT)

        def products(s):
            two = psum[0:NP, (4 + 2 * (s % 2)) * 512:(6 + 2 * (s % 2)) * 512]
            two = two.rearrange("p (h x) -> p h x", h=2)[:, :, 0:4 * D].rearrange("p h (t w) -> p h t w", t=2)
            return two[:, :, :, 0:D], two[:, :, :, D:2 * D]

        def paired(t, g):
            return group_of(t, g).rearrange("p (h t) d -> p h t d", h=2)

        def slot(s):
            return gbuf[1][0:NP, s * GT:(s + 1) * GT, :]

        block = ctx.enter_context(nc.Block())

        @block.sync
        def _(sp):
            def load_indices(k, c, i, b, u, col):
                sp.wait_ge(s_gath[k][b], i * (16 * U))
                sp.dma_start(idx[b][:, 0:u], src_v[:, bass.ds(col, u)]).then_inc(s_idx[k][b], 16)

            def load_edges(k, c, i, b, u):
                sp.wait_ge(s_q[k], c * QG)
                if u == U:
                    sp.dma_start(ea[b][:, :, :], ea_main[bass.ds(c, 1)].rearrange("a k q p -> (a k) q p")) \
                        .then_inc(s_ea[k][b], 16)
                else:
                    sp.dma_start(ea[b][:, 0, :], ea_tail).then_inc(s_ea[k][b], 16)
                    sp.dma_start(ea[b][0:DE, 1, :], ea_last).then_inc(s_ea[k][b], 16)

            def store_table(k):
                with sp.Fori(0, GLOOPS) as i:
                    sp.wait_ge(s_pe[k], i * GBODY + GBODY + 2)
                    at = bass.ds(i * (GBODY * GT), GBODY * GT)
                    node_dma(sp, table_v[:, at, :], R[:, at, :], s_tab[k])
                sp.wait_ge(s_pe[k], GROUPS + 2)
                node_dma(sp, table_v[:, TILES - GT:TILES, :], R[:, TILES - GT:TILES, :], s_tab[k])

            for n in range(5):
                at = slice(n * XT, (n + 1) * XT)
                node_dma(sp, X[:, at, :], x_v[:, at, :], s_x[n])
            sp.dma_start(dst_i, dst_v).then_inc(s_dst, 16)
            sp.dma_start(first_i[:, :], dst_v[:, 0:1], allow_slow_non_contiguous=True).then_inc(s_edge, 16)
            sp.wait_ge(s_clear, 5)
            sp.dma_start(prev_i[1:P, :], dst_v[0:P - 1, EP - 1:EP],
                         allow_slow_non_contiguous=True).then_inc(s_edge, 16)
            for n in range(5):
                at = slice(n * XT, (n + 1) * XT)
                sp.wait_ge(s_h0, (n + 1) * XT)
                node_dma(sp, table_v[:, at, :], R[:, at, :], s_tab[0])
            chunks(sp, lambda c, i, b, u, col: load_indices(0, c, i, b, u, col))
            sp.wait_ge(s_lastf, 1)
            sp.dma_start(last_v, last_f[:, :]).then_inc(s_lastd, 16)
            for k in (1, 2):
                store_table(k)
                for b in range(2):
                    sp.wait_ge(s_gath[k - 1][b], 16 * (U * CLOOPS + (LASTU if b == 0 else 0)))

                def load(c, i, b, u, col, k=k):
                    load_indices(k, c, i, b, u, col)
                    load_edges(k, c, i, b, u)
                chunks(sp, load)
            with sp.Fori(0, GLOOPS) as i:
                sp.wait_ge(s_c2, (i * GBODY + GBODY) * 3)
                at = bass.ds(i * (GBODY * GT), GBODY * GT)
                node_dma(sp, out_v[:, at, :], X[:, at, :], s_out)
            sp.wait_ge(s_c2, GROUPS * 3)
            node_dma(sp, out_v[:, TILES - GT:TILES, :], X[:, TILES - GT:TILES, :], s_out)
            sp.wait_ge(s_out, 32 * (GLOOPS + 1))

        @block.gpsimd
        def _(pool):
            pool.memset(ident[:, :], 0.0).then_inc(s_const, 1)
            pool.memset(ones[:, :], 1.0).then_inc(s_const, 1)
            pool.memset(zero16[:, :], 0.0).then_inc(s_hist0, 1)
            pool.wait_ge(s_const, 2)
            pool.affine_select(out=ident[:, :], in_=ident[:, :], compare_op=ALU.not_equal, fill=1.0,
                               base=0, pattern=[[-1, P]], channel_multiplier=1).then_inc(s_const, 1)
            pool.affine_select(out=below[:, :], in_=ones[:, :], compare_op=ALU.is_gt, fill=0.0,
                               base=0, pattern=[[1, P]], channel_multiplier=-1).then_inc(s_const, 1)
            pool.iota(ramp_i[:, :], pattern=[[1, P]], base=0, channel_multiplier=0).then_inc(s_const, 1)
            pool.iota(chain_end_i[:, :], pattern=[[0, 1]], base=EP - 1, channel_multiplier=EP) \
                .then_inc(s_const, 1)

            def gather(k, c, i, b, u, col):
                pool.wait_ge(s_idx[k][b], i * 16 + 16)
                pool.wait_ge(s_wrote[k][b], i * 16)
                pool.sem_inc(s_go, 1)
                for n in range(u):
                    pool.indirect_dma_start(
                        out=gbuf[b][:, n, :], out_offset=None, in_=table[:, :],
                        in_offset=bass.IndirectOffsetOnAxis(ap=idx[b][:, n:n + 1], axis=0)) \
                        .then_inc(s_gath[k][b], 16)

            def fetch(k, g, s):
                pool.wait_ge(s_slot[k], g * 2 + 2)
                pool.sem_inc(s_go, 1)
                for t in range(GT):
                    pool.indirect_dma_start(
                        out=slot(s)[:, t, :], out_offset=None, in_=states[:, :],
                        in_offset=bass.IndirectOffsetOnAxis(ap=lidx[s][:, t:t + 1], axis=0),
                        bounds_check=E - 1, oob_is_err=False).then_inc(s_ext[k][s], 16)

            for k in range(3):
                pool.wait_ge(s_tab[k], TABLE_DONE[k])
                if k:
                    pool.wait_ge(s_slot[k - 1], 2 * (GROUPS + GBODY))
                chunks(pool, lambda c, i, b, u, col, k=k: gather(k, c, i, b, u, col))
                if k == 0:
                    pool.wait_ge(s_lastd, 16)
                    pool.wait_ge(s_edge, 32)
                    pool.indirect_dma_start(
                        out=first_last[:, :], out_offset=None, in_=last_dram[:, :],
                        in_offset=bass.IndirectOffsetOnAxis(ap=first_i[:, :], axis=0),
                        bounds_check=N - 1, oob_is_err=False).then_inc(s_flast, 16)
                    pool.wait_ge(s_fixi, 1)
                pool.wait_ge(s_wrote[k][0], 16 * (CLOOPS + 1))
                pool.wait_ge(s_wrote[k][1], 16 * CLOOPS)
                pool.wait_ge(s_fixz[k], 1)
                pool.indirect_dma_start(
                    out=fix_rows[:, :], out_offset=None, in_=states[:, :],
                    in_offset=bass.IndirectOffsetOnAxis(ap=fix_i[:, :], axis=0),
                    bounds_check=E - 1, oob_is_err=False).then_inc(s_fixg[k], 16)
                pool.wait_ge(s_fixed[k], 1)
                pool.indirect_dma_start(
                    out=states[:, :], out_offset=bass.IndirectOffsetOnAxis(ap=fix_i[:, :], axis=0),
                    in_=fix_rows[:, :], in_offset=None,
                    bounds_check=E - 1, oob_is_err=False).then_inc(s_fixw[k], 16)
                pool.wait_ge(s_fixw[k], 16)
                groups(pool, lambda g, s, i, k=k: fetch(k, g, s))

        @block.scalar
        def _(act):
            for to, of in ((Wl, wlT), (Wr, wrT)):
                act.dma_start(to[:, :], of).then_inc(s_w, 16)
            for n, of in enumerate((bl, gamma, beta)):
                act.dma_start(cols[:, n:n + 1], of.rearrange("(d a) -> d a", a=1)).then_inc(s_w, 16)
            act.wait_ge(s_clear, 5)
            for k, msg, root, bias in ((1, w1_msg, w1_root, b1), (2, w2_msg, w2_root, b2)):
                act.dma_start(Wmo[k][0:D, 0:D], msg).then_inc(s_w, 16)
                act.dma_start(Wmo[k][0:D, D:2 * D], root).then_inc(s_w, 16)
                act.dma_start(Wmo[k][D:D + 1, D:2 * D], bias.rearrange("(a d) -> a d", a=1)).then_inc(s_w, 16)
            for to, of in ((We[1], w1_edge), (We[2], w2_edge)):
                for n in range(4):
                    act.dma_start(to[n * DE:(n + 1) * DE, n * D:(n + 1) * D], of).then_inc(s_w, 16)

            for n in range(6):
                if n < 5:
                    at = slice(n * XT, (n + 1) * XT)
                    act.wait_ge(s_var, n + 1)
                    nc.scalar.activation(ln_a[:, at], ln_b[:, at], ACT.Sqrt, scale=1.0 / D,
                                         bias=eps[0:NP, :]).then_inc(s_std, 1)
                if n:
                    act.wait_ge(s_norm, n)
                    with act.Fori(0, XT // 4) as i:
                        for n4 in range(4):
                            t = i * 4 + ((n - 1) * XT + n4)
                            nc.scalar.activation(
                                R[:, bass.ds(t, 1), :].rearrange("p a d -> p (a d)"),
                                X[:, bass.ds(t, 1), :].rearrange("p a d -> p (a d)"), ACT.Relu,
                                bias=shift[:, bass.ds(t, 1)], scale=rstd[:, bass.ds(t, 1)]).then_inc(s_h0, 1)

            def stage_mask(k, b, u, col):
                if k == 0:
                    nc.scalar.copy(mask[b][:, 0:u], same[:, bass.ds(col, u)]).then_inc(s_mask[k], 1)
                else:
                    nc.scalar.activation(mask[b][:, 0:u], same[:, bass.ds(col, u)], ACT.Copy,
                                         scale=BIG, bias=-BIG).then_inc(s_mask[k], 1)

            def store_states(k, c, b, u, col):
                act.wait_ge(s_chain[k], c * STEPS + u + 1)
                act.dma_start(states_v[:, bass.ds(col, u), :], gbuf[b][:, 0:u, :]).then_inc(s_wrote[k][b], 16)

            def states_pass(k):
                with act.Fori(0, CLOOPS) as i:
                    for b in range(2):
                        stage_mask(k, b, U, i * (2 * U) + b * U)
                    for b in range(2):
                        store_states(k, i * 2 + b, b, U, i * (2 * U) + b * U)
                stage_mask(k, 0, LASTU, LASTCOL)
                store_states(k, 2 * CLOOPS, 0, LASTU, LASTCOL)

            def copy_products(g, s, i):
                act.wait_ge(s_tA[2], g + 3)
                nc.scalar.copy(featA[s % 2][0:D, :], wide(s % 2)).then_inc(s_eA[2], 1)
                act.wait_ge(s_pm[2], g + 1)
                nc.scalar.copy(paired(R, g), products(s)[0]).then_inc(s_pe[2], 1)
                nc.scalar.copy(paired(ROOT, g), products(s)[1]).then_inc(s_re[2], 1)

            act.wait_ge(s_same, 1)
            states_pass(0)

            def first_layer(g, s, i):
                act.wait_ge(s_tB, g + 1)
                nc.scalar.copy(nodeB[s % 2][:, :, :], group_of(R, g)).then_inc(s_nB, 1)
                act.wait_ge(s_tA[0], g + 3)
                nc.scalar.copy(featA[s % 2][0:D, :], wide(s % 2)).then_inc(s_eA[0], 1)
                act.wait_ge(s_mm, g + 1)
                nc.scalar.activation(ft_of(g), wide(4 + s % 2), ACT.Identity,
                                     bias=cols[:, 0:1]).then_inc(s_ft, 1)
            act.wait_ge(s_w, 16 * N_W)
            groups(act, first_layer)
            act.wait_ge(s_bvar, 1)
            nc.scalar.activation(bstd[:, :], bmv[:, 1:2], ACT.Sqrt, bias=eps[0:D, :]).then_inc(s_bstd, 1)
            act.wait_ge(s_bn, 1)

            def batch_norm(g, s, i):
                act.wait_ge(s_yT, g + 1)
                nc.scalar.activation(featA[s % 2][0:D, :], ft_of(g), ACT.Relu, bias=bshift[:, :],
                                     scale=bscale[:, :]).then_inc(s_y, 1)
            groups(act, batch_norm)
            act.wait_ge(s_var, 6)
            nc.scalar.activation(ln_a[:, :], ln_b[:, :], ACT.Sqrt, scale=1.0 / D,
                                 bias=eps[0:NP, :]).then_inc(s_std, 1)
            act.wait_ge(s_norm, 6)

            def second_norm(g, s, i):
                act.wait_ge(s_tA[1], g + 1)
                for t in range(GT):
                    at = bass.ds(g * GT + t, 1)
                    nc.scalar.activation(nodeA[s % 2][:, t, :], X[:, at, :].rearrange("p a d -> p (a d)"),
                                         ACT.Relu, bias=shift[:, at], scale=rstd[:, at]).then_inc(s_h1, 1)
            groups(act, second_norm)
            states_pass(1)
            act.wait_ge(s_tab[1], TABLE_DONE[1])
            groups(act, copy_products)
            states_pass(2)

        @block.tensor
        def _(pe):
            pe.sem_inc(s_ohmul, 2)
            pe.sem_inc(s_tA[0], 2)
            pe.sem_inc(s_tA[1], 2)
            pe.sem_inc(s_tA[2], 2)
            pe.sem_inc(s_yT, 2)
            pe.sem_inc(s_tB, 2)
            pe.sem_inc(s_q[1], QG)
            pe.sem_inc(s_q[2], QG)

            def transpose_nodes(b, tile, done):
                for t in range(GT):
                    last = nc.tensor.transpose(bank[b][0:D, t * NP:(t + 1) * NP], tile(t), ident[0:NP, 0:NP])
                last.then_inc(done, 1)

            def chain_tails(k):
                pe.wait_ge(s_chain[k], CHAIN_ALL)
                nc.tensor.transpose(bank[6][0:D, 0:P], gbuf[0][:, LASTU - 1, :], ident[:, :]).then_inc(s_tail[k], 1)
                pe.wait_ge(s_scan[k], 1)
                nc.tensor.transpose(bank[7][:, 0:D], chainT[:, 0:P], ident[0:D, 0:D]).then_inc(s_back[k], 1)

            pe.wait_ge(s_hist0, 1)
            nc.tensor.matmul(HIST, zero16[:, 0:NP], zero16[:, 0:TILES], start=True, stop=False,
                             skip_group_check=True)

            def histogram(c, i, b, u, col):
                pe.wait_ge(s_oh, c * 2 + 2)
                for n in range(u):
                    last = nc.tensor.matmul(HIST, oh_hi[b][:, n, :], oh_lo[b][:, n, :], start=False,
                                            stop=(u == LASTU and n == u - 1), skip_group_check=True)
                last.then_inc(s_ohmul if u == U else s_hist, 1)
            chunks(pe, histogram)
            pe.wait_ge(s_const, 6)
            pe.wait_ge(s_upto, 1)
            nc.tensor.matmul(bank[6][0:NP, 0:1], below[0:NP, 0:NP], upto[:, TILES - 1:TILES],
                             start=True, stop=True).then_inc(s_prefix, 1)
            pe.wait_ge(s_diag, 1)
            nc.tensor.matmul(bank[5][0:D, 0:P], ones[:, 0:D], diag[:, :], start=True, stop=True).then_inc(s_span, 1)
            chain_tails(0)
            pe.wait_ge(s_w, 16 * N_W)

            def first_layer(g, s, i):
                pe.wait_ge(s_eB, g + 1)
                pe.wait_ge(s_nB, g + 1)
                transpose_nodes(2 + s % 2, lambda t: nodeB[s % 2][:, t, :], s_tB)
                pe.wait_ge(s_mean, g + 1)
                pe.wait_ge(s_eA[0], g + 1)
                transpose_nodes(s % 2, lambda t: nodeA[s % 2][:, t, :], s_tA[0])
                pe.wait_ge(s_eA[0], g + 3)
                pe.wait_ge(s_eB, g + 3)
                pe.wait_ge(s_ft, g + 1)
                nc.tensor.matmul(wide(4 + s % 2), Wl[:, :], featA[s % 2][0:D, :], start=True, stop=False)
                nc.tensor.matmul(wide(4 + s % 2), Wr[:, :], featB[s % 2][:, :], start=False, stop=True) \
                    .then_inc(s_mm, 1)
            groups(pe, first_layer)

            def back_to_nodes(g, s, i):
                pe.wait_ge(s_y, g + 1)
                pe.wait_ge(s_x1, g + 1)
                for t in range(GT):
                    last = nc.tensor.transpose(bank[s % 2][0:NP, t * D:(t + 1) * D],
                                               featA[s % 2][0:D, t * NP:(t + 1) * NP], ident[0:D, 0:D])
                last.then_inc(s_yT, 1)
            groups(pe, back_to_nodes)

            def messages(k, g, s, source, per_group):
                pe.wait_ge(source, g * per_group + per_group)
                pe.wait_ge(s_eA[k], g + 1)
                transpose_nodes(s % 2, lambda t: nodeA[s % 2][:, t, :], s_tA[k])
                pe.wait_ge(s_eA[k], g + 3)
                pe.wait_ge(s_pe[k], g + 1)
                pe.wait_ge(s_re[k], g + 1)
                for t in range(GT):
                    first = (4 + 2 * (s % 2) + t // 2) * 512 + t % 2 * 2 * D
                    last = nc.tensor.matmul(psum[0:NP, first:first + 2 * D],
                                            featA[s % 2][:, t * NP:(t + 1) * NP], Wmo[k][:, :],
                                            start=True, stop=True)
                last.then_inc(s_pm[k], 1)

            def edge_products(k, c, i, b, u):
                pe.wait_ge(s_ea[k][b], i * 16 + (16 if u == U else 32))
                for q in range(QG if u == U else LASTQ):
                    pe.wait_ge(s_qadd[k], c * QG + (q + 1))
                    if u == U or q == 0:
                        nc.tensor.matmul(bank[q][:, 0:4 * D], ea[b][:, q, :], We[k][:, :],
                                         start=True, stop=True).then_inc(s_q[k], 1)
                    else:
                        nc.tensor.matmul(bank[q][:, 0:D], ea[b][0:DE, q, :], We[k][0:DE, 0:D],
                                         start=True, stop=True).then_inc(s_q[k], 1)

            for k in (1, 2):
                source, per_group = ((s_h1, GT), (s_c, 2))[k - 1]
                groups(pe, lambda g, s, i: messages(k, g, s, source, per_group))
                pe.wait_ge(s_pe[k], GROUPS + 2)
                pe.wait_ge(s_re[k], GROUPS + 2)
                chunks(pe, lambda c, i, b, u, col: edge_products(k, c, i, b, u))
                chain_tails(k)

        @block.vector
        def _(dve):
            steps = [0]

            def link(ins):
                steps[0] += 1
                ins.then_inc(s_v, 1)
                dve.wait_ge(s_v, steps[0])

            tt, ts, stt = nc.vector.tensor_tensor, nc.vector.tensor_scalar, nc.vector.scalar_tensor_tensor
            copy, memset = nc.vector.tensor_copy, nc.vector.memset
            for ring, size in ((s_eA[1], 2), (s_eB, 2), (s_x1, 2), (s_pe[1], 2), (s_re[1], 2), (s_re[2], 2),
                               (s_qadd[1], QG), (s_qadd[2], QG), (s_eA[0], 2), (s_eA[2], 2), (s_ft, 2),
                               (s_pe[2], 2)):
                dve.sem_inc(ring, size)
            memset(We[1][:, :], 0.0).then_inc(s_clear, 1)
            memset(We[2][:, :], 0.0).then_inc(s_clear, 1)
            memset(prev_i[:, :], -1).then_inc(s_clear, 1)
            memset(Wmo[1][D:D + 1, :], 0.0).then_inc(s_clear, 1)
            memset(Wmo[2][D:D + 1, :], 0.0).then_inc(s_clear, 1)
            for k in range(2):
                link(memset(featA[k][D:D + 1, :], 1.0))
            link(memset(eps[:, :], EPS))

            def variance(at):
                w = [stats[:, at, f:f + 1].rearrange("p t a -> p (t a)") for f in range(6)]
                a, b, c, d = (t[:, at] for t in (ln_d, ln_b, ln_c, shift))
                link(tt(a, w[1], w[4], ALU.subtract))
                link(tt(c, w[1], w[4], ALU.add))
                link(tt(d, w[2], w[5], ALU.add))
                link(tt(b, a, a, ALU.mult))
                stt(out=b, in0=b, scalar=D / 4.0, in1=d, op0=ALU.mult, op1=ALU.add).then_inc(s_var, 1)

            def scale_and_shift(at, n):
                dve.wait_ge(s_std, n)
                link(nc.vector.reciprocal(rstd[:, at], ln_a[:, at]))
                stt(out=shift[:, at], in0=ln_c[:, at], scalar=-0.5, in1=rstd[:, at], op0=ALU.mult,
                    op1=ALU.mult).then_inc(s_norm, 1)

            for n in range(5):
                dve.wait_ge(s_x[n], 32)
                with dve.Fori(0, XT // 4) as i:
                    for n4 in range(4):
                        at = bass.ds(i * 4 + (n * XT + n4), 1)
                        nc.vector.bn_stats(stats[:, at, :].rearrange("p a f -> p (a f)"),
                                           X[:, at, :].rearrange("p a d -> p (a d)")).then_inc(s_bnsraw, 1)
                dve.wait_ge(s_bnsraw, (n + 1) * XT)
                variance(slice(n * XT, (n + 1) * XT))
                if n:
                    scale_and_shift(slice((n - 1) * XT, n * XT), n)
            scale_and_shift(slice(4 * XT, 5 * XT), 5)

            dve.wait_ge(s_dst, 16)
            link(copy(dst_f, dst_i))
            link(ts(quot_i, dst_f, 1.0 / TILES, None, ALU.mult))
            link(copy(quot_f, quot_i))
            link(stt(out=rest_f, in0=quot_f, scalar=-float(TILES), in1=dst_f, op0=ALU.mult, op1=ALU.add))
            for test, bound, up in ((ALU.is_ge, float(TILES), 1.0), (ALU.is_lt, 0.0, -1.0)):
                link(ts(same[:, :], rest_f, bound, None, test))
                link(stt(out=quot_f, in0=same[:, :], scalar=up, in1=quot_f, op0=ALU.mult, op1=ALU.add))
                link(stt(out=rest_f, in0=same[:, :], scalar=-up * TILES, in1=rest_f, op0=ALU.mult, op1=ALU.add))
            link(copy(hi, quot_f))
            link(copy(lo, rest_f))
            link(memset(same[:, 0:1], 0.0))
            tt(same[:, 1:EP], dst_f[:, 1:EP], dst_f[:, 0:EP - 1], ALU.is_equal).then_inc(s_same, 1)
            dve.wait_ge(s_edge, 32)
            dve.wait_ge(s_const, 6)
            link(copy(first_f[:, :], first_i[:, :]))
            link(copy(prev_f[:, :], prev_i[:, :]))
            link(copy(chain_end[:, :], chain_end_i[:, :]))
            link(tt(joins[:, :], first_f[:, :], prev_f[:, :], ALU.is_equal))
            link(tt(spans[:, :], first_f[:, :], dst_f[:, EP - 1:EP], ALU.is_equal))
            link(tt(spans[:, :], spans[:, :], joins[:, :], ALU.mult))
            ts(diag[:, :], ident[:, :], spans[:, 0:1], None, ALU.mult).then_inc(s_diag, 1)
            link(copy(ramp[:, :], ramp_i[:, :]))
            link(memset(first_last[:, :], NOWHERE))
            link(memset(last_i[:, :], 0))
            link(memset(chainT[:, 0:1], 0.0))

            def last_edges():
                dve.wait_ge(s_hist, 1)
                link(copy(hist[:, :], HIST))
                link(nc.vector.tensor_tensor_scan(out=upto[:, :], data0=ones[0:NP, 0:TILES], data1=hist[:, :],
                                                  initial=0.0, op0=ALU.mult, op1=ALU.add))
                dve.sem_inc(s_upto, 1)
                link(ts(empty[:, :], hist[:, :], 0.0, None, ALU.is_equal))
                link(ts(hist[:, :], hist[:, :], 1.0, None, ALU.max))
                link(nc.vector.reciprocal(inv_deg[:, :], hist[:, :]))
                dve.wait_ge(s_prefix, 1)
                link(copy(prefix[:, :], bank[6][0:NP, 0:1]))
                link(ts(last_f[:, :], upto[:, :], prefix[:, 0:1], -1.0, ALU.add, ALU.add))
                stt(out=last_f[:, :], in0=empty[:, :], scalar=NOWHERE, in1=last_f[:, :], op0=ALU.mult,
                    op1=ALU.add).then_inc(s_lastf, 1)
                dve.wait_ge(s_lastf, 1)
                link(copy(last_i[:, 0:TILES], last_f[:, :]))
                dve.wait_ge(s_span, 1)
                link(copy(span_mul[:, :], bank[5][0:D, 0:P]))
                link(ts(span_add[:, :], span_mul[:, :], -1.0, BIG, ALU.add, ALU.mult))

            def chain(k, c, i, b, u, col):
                if k == 0:
                    dve.wait_ge(s_ohmul, c + 1)
                    for to, of, w in ((oh_hi[b], hi, NP), (oh_lo[b], lo, TILES)):
                        tt(to[:, 0:u, :], ramp[:, 0:w].unsqueeze(1).to_broadcast([P, u, w]),
                           of[:, bass.ds(col, u)].unsqueeze(2).to_broadcast([P, u, w]), ALU.is_equal) \
                            .then_inc(s_oh, 1)
                    if u == LASTU:
                        last_edges()
                dve.wait_ge(s_gath[k][b], i * (16 * U) + 16 * u)
                if k:
                    for q in range(QG if u == U else LASTQ):
                        dve.wait_ge(s_q[k], c * QG + (q + 1 + QG))
                        n = min(4, u - 4 * q)
                        rows = gbuf[b][:, 4 * q:4 * q + n, :].rearrange("p n d -> p (n d)")
                        tt(rows, rows, bank[q][:, 0:n * D], ALU.add).then_inc(s_qadd[k], 1)
                dve.wait_ge(s_mask[k], c + 1)
                ops = (ALU.mult, ALU.add) if k == 0 else (ALU.add, ALU.max)
                before = carry[:, :]
                for n in range(u):
                    if k and n % 4 == 0:
                        dve.wait_ge(s_qadd[k], c * QG + (n // 4 + 1 + QG))
                    dve.wait_ge(s_chain[k], c * STEPS + n)
                    row = gbuf[b][:, n, :]
                    stt(out=row, in0=before, scalar=mask[b][:, n:n + 1], in1=row, op0=ops[0], op1=ops[1]) \
                        .then_inc(s_chain[k], 1)
                    before = row
                dve.wait_ge(s_chain[k], c * STEPS + u)
                copy(carry[:, :], before).then_inc(s_chain[k], 1)

            def complete_segments(k):
                memset(fix_rows[:, :], 0.0).then_inc(s_fixz[k], 1)
                if k == 0:
                    dve.wait_ge(s_flast, 16)
                    link(tt(fix_ok[:, :], first_last[:, :], chain_end[:, :], ALU.is_le))
                    link(tt(fix_ok[:, :], fix_ok[:, :], joins[:, :], ALU.mult))
                    link(ts(fix_f[:, :], first_last[:, :], -NOWHERE, fix_ok[:, 0:1], ALU.add, ALU.mult))
                    ts(fix_i[:, :], fix_f[:, :], NOWHERE, None, ALU.add).then_inc(s_fixi, 1)
                dve.wait_ge(s_tail[k], 1)
                nc.vector.tensor_tensor_scan(
                    out=chainT[:, 1:P + 1], data0=(span_add if k else span_mul)[:, :],
                    data1=bank[6][0:D, 0:P], initial=0.0, op0=ALU.add if k else ALU.mult,
                    op1=ALU.max if k else ALU.add).then_inc(s_scan[k], 1)
                for s in range(GBODY):
                    if s == 0:
                        dve.wait_ge(s_wrote[k][1], 16 * CLOOPS)
                    prepare(k, s, s)
                dve.wait_ge(s_fixg[k], 16)
                dve.wait_ge(s_back[k], 1)
                tt(fix_rows[:, :], fix_rows[:, :], bank[7][:, 0:D], ALU.max if k else ALU.add) \
                    .then_inc(s_fixed[k], 1)

            def prepare(k, g, s):
                memset(slot(s), 0.0).then_inc(s_slot[k], 1)
                copy(lidx[s][:, :], last_i[:, bass.ds(g * GT, GT)]).then_inc(s_slot[k], 1)

            def fetched(k, s, i):
                dve.wait_ge(s_ext[k][s], i * (16 * GT) + 16 * GT)

            link(memset(carry[:, :], 0.0))
            chunks(dve, lambda c, i, b, u, col: chain(0, c, i, b, u, col))
            complete_segments(0)

            def means(g, s, i):
                fetched(0, s, i)
                tt(nodeA[s % 2][:, :, :], slot(s),
                   inv_deg[:, bass.ds(g * GT, GT)].unsqueeze(2).to_broadcast([NP, GT, D]), ALU.mult) \
                    .then_inc(s_mean, 1)
                dve.wait_ge(s_mean, g + 1)
                prepare(0, g + GBODY, s)
                dve.wait_ge(s_tB, g + 3)
                copy(featB[s % 2][:, :], wide(2 + s % 2)).then_inc(s_eB, 1)
                if s == GBODY - 1:
                    for r in range(GBODY):
                        at = i * GBODY + r
                        dve.wait_ge(s_ft, at + 3)
                        nc.vector.bn_stats(bstats[:, bass.ds(at, 1), :].rearrange("p a f -> p (a f)"),
                                           ft_of(at)).then_inc(s_bst, 1)
            groups(dve, means)
            dve.wait_ge(s_ft, GROUPS + 2)
            nc.vector.bn_stats(bstats[:, GROUPS - 1, :], ft_of(GROUPS - 1)).then_inc(s_bst, 1)
            dve.wait_ge(s_bst, GROUPS)
            nc.vector.bn_aggr(bmv[:, :], bstats[:, :, :].rearrange("p g f -> p (g f)")).then_inc(s_bvar, 1)
            dve.wait_ge(s_bstd, 1)
            dve.wait_ge(s_w, 16 * N_W)
            link(nc.vector.reciprocal(bstd[:, :], bstd[:, :]))
            link(tt(bscale[:, :], bstd[:, :], cols[:, 1:2], ALU.mult))
            link(tt(bshift[:, :], bmv[:, 0:1], bscale[:, :], ALU.mult))
            tt(bshift[:, :], cols[:, 2:3], bshift[:, :], ALU.subtract).then_inc(s_bn, 1)

            def add_first_layer(g, s, i):
                dve.wait_ge(s_yT, g + 3)
                tt(group_of(X, g), group_of(X, g), narrow(s % 2), ALU.add).then_inc(s_x1, 1)
                dve.wait_ge(s_x1, g + 3)
                for t in range(GT):
                    at = bass.ds(g * GT + t, 1)
                    nc.vector.bn_stats(stats[:, at, :].rearrange("p a f -> p (a f)"),
                                       X[:, at, :].rearrange("p a d -> p (a d)")).then_inc(s_bnsraw, 1)
            groups(dve, add_first_layer)
            dve.wait_ge(s_bnsraw, 2 * TILES)
            variance(slice(0, TILES))
            scale_and_shift(slice(0, TILES), 6)

            def copy_products(g, s, i):
                dve.wait_ge(s_tA[1], g + 3)
                copy(featA[s % 2][0:D, :], wide(s % 2)).then_inc(s_eA[1], 1)
                dve.wait_ge(s_pm[1], g + 1)
                copy(paired(R, g), products(s)[0]).then_inc(s_pe[1], 1)
                copy(paired(ROOT, g), products(s)[1]).then_inc(s_re[1], 1)
            dve.wait_ge(s_tab[0], TABLE_DONE[0])
            groups(dve, copy_products)

            def max_pass(k):
                link(memset(carry[:, :], 0.0))
                chunks(dve, lambda c, i, b, u, col: chain(k, c, i, b, u, col))
                dve.wait_ge(s_re[k], GROUPS + 2)
                complete_segments(k)

            max_pass(1)

            def first_conv(g, s, i):
                fetched(1, s, i)
                dve.wait_ge(s_tA[2], g + 1)
                tt(nodeA[s % 2][:, :, :], slot(s), group_of(ROOT, g), ALU.add).then_inc(s_c, 1)
                dve.wait_ge(s_c, g * 2 + 1)
                stt(out=nodeA[s % 2][:, :, :], in0=nodeA[s % 2][:, :, :], scalar=SLOPE,
                    in1=nodeA[s % 2][:, :, :], op0=ALU.mult, op1=ALU.max).then_inc(s_c, 1)
                prepare(1, g + GBODY, s)
            groups(dve, first_conv)
            max_pass(2)

            def second_conv(g, s, i):
                fetched(2, s, i)
                tt(nodeA[s % 2][:, :, :], slot(s), group_of(ROOT, g), ALU.add).then_inc(s_c2, 1)
                dve.wait_ge(s_c2, g * 3 + 1)
                stt(out=nodeA[s % 2][:, :, :], in0=nodeA[s % 2][:, :, :], scalar=SLOPE,
                    in1=nodeA[s % 2][:, :, :], op0=ALU.mult, op1=ALU.max).then_inc(s_c2, 1)
                dve.wait_ge(s_c2, g * 3 + 2)
                tt(group_of(X, g), group_of(X, g), nodeA[s % 2][:, :, :], ALU.add).then_inc(s_c2, 1)
                prepare(2, g + GBODY, s)
            groups(dve, second_conv)


def kernel(**inputs):
    import numpy as np
    import concourse.bacc as bacc
    from concourse.bass_utils import run_bass_kernel_spmd

    nc = bacc.Bacc("TRN2", target_bir_lowering=False, num_devices=1)
    given = {k: np.asarray(v) for k, v in inputs.items()}
    ea = given["edge_attr_32"].reshape(P, EP, DE)
    main = ea[:, :LASTCOL].reshape(P, 2 * CLOOPS, QG, 4, DE).transpose(1, 3, 4, 2, 0)
    tail = ea[:, LASTCOL:LASTCOL + 4].reshape(P, 4 * DE).transpose(1, 0)
    arrays = {
        "x": given["x"], "src": given["src"], "dst": given["dst"],
        "ea_main": main.reshape(2 * CLOOPS, 4 * DE, QG, P), "ea_tail": tail,
        "ea_last": ea[:, EP - 1].transpose(1, 0),
        "wlT": given["L0_gnn_Wl"].T, "bl": given["L0_gnn_bl"], "wrT": given["L0_gnn_Wr"].T,
        "gamma": given["L0_gnn_gamma"], "beta": given["L0_gnn_beta"],
    }
    for layer in "12":
        for name, key in (("msg", "W{}_msg"), ("edge", "W{}_edge"), ("root", "W{}_root")):
            arrays[f"w{layer}_{name}"] = given["L1_gnn_" + key.format(layer)]
        arrays[f"b{layer}"] = given[f"L1_gnn_b{layer}"]
    arrays = {f"in_{k}": np.ascontiguousarray(v) for k, v in arrays.items()}
    args = {k[3:]: nc.dram_tensor(k, a.shape, mybir.dt.from_np(a.dtype), kind="ExternalInput").ap()
            for k, a in arrays.items()}
    out = nc.dram_tensor("out_0", (N, D), F32, kind="ExternalOutput").ap()
    gnn_kernel(nc, out=out, **args)
    r = run_bass_kernel_spmd(nc, [arrays], core_ids=[0])
    return r.results[0]["out_0"]
```

```python
import concourse.bass as bass
from concourse import mybir
from contextlib import ExitStack

F32 = mybir.dt.float32
BF16 = mybir.dt.bfloat16
I32 = mybir.dt.int32
ALU = mybir.AluOpType
ACT = mybir.ActivationFunctionType

N, D, E, DE = 12500, 96, 400000, 32
P = 128
EP = E // P
NP = 125
TILES = N // NP
GT = 4
GROUPS = TILES // GT
GCOLS = GT * NP
GBODY = 4
GLOOPS = GROUPS // GBODY
U = 24
CLOOPS = EP // (2 * U)
LASTU = EP - 2 * U * CLOOPS
UH = U // 2
QG = U // 4
LASTCOL = EP - LASTU
BIG = 3.0e38
NOWHERE = float(1 << 23)
NWIDE = 112
EPS = 1e-5
SLOPE = 0.01
N_W = 19

assert GROUPS == GBODY * GLOOPS + 1 and NP * TILES == N and EP * P == E and LASTU == 5


def gnn_kernel(nc, x, src, dst, ea_main, ea_tail, ea_last, wlT, bl, wrT, gamma, beta,
               w1_msg, w1_edge, w1_root, b1, w2_msg, w2_edge, w2_root, b2, out):
    ctx = ExitStack()
    with ctx:
        def sb(name, shape, dt=F32):
            return ctx.enter_context(nc.sbuf_tensor(name, shape, dt))

        def sem(name):
            return ctx.enter_context(nc.semaphore(name))

        table = nc.dram_tensor("table", (N, D), F32, kind="Internal").ap()
        states = nc.dram_tensor("states", (E, D), F32, kind="Internal").ap()
        last_dram = nc.dram_tensor("last_dram", (N, 1), F32, kind="Internal").ap()
        x_v = x.rearrange("(p t) d -> p t d", p=NP)
        out_v = out.rearrange("(p t) d -> p t d", p=NP)
        table_v = table.rearrange("(p t) d -> p t d", p=NP)
        states_v = states.rearrange("(p j) d -> p j d", p=P)
        last_v = last_dram.rearrange("(p t) a -> p (t a)", p=NP)
        src_v = src.rearrange("(p j) -> p j", p=P)
        dst_v = dst.rearrange("(p j) -> p j", p=P)

        X = sb("X", [NP, TILES, D])
        R = sb("R", [NP, TILES, D])
        FT = sb("FT", [P, GROUPS * GCOLS])
        OWN = FT[0:NP, 0:TILES * D].rearrange("p (t d) -> p t d", t=TILES)
        same = sb("same", [P, EP])
        gbuf = [sb(f"gbuf{b}", [P, U, D]) for b in range(2)]
        idx = [sb(f"idx{b}", [P, U], I32) for b in range(2)]
        mask = [sb(f"mask{b}", [P, U]) for b in range(2)]
        ea = [sb(f"ea{b}", [P, QG * P])[:, :] for b in range(2)]
        ea_q = [e.rearrange("p (q c) -> p q c", q=QG) for e in ea]
        carry = sb("carry", [P, D])
        lidx = [sb(f"lidx{s}", [P, GT], I32) for s in range(GBODY)]
        nodeA = [sb(f"nodeA{k}", [NP, GT, D]) for k in range(2)]
        featA = [sb(f"featA{k}", [D + 1, GCOLS]) for k in range(2)]
        hi = sb("hi", [P, EP], BF16)
        lo = sb("lo", [P, EP], BF16)
        oh_hi = [sb(f"oh_hi{b}", [P, UH, NP], BF16) for b in range(2)]
        oh_lo = [ea[b].bitcast(BF16)[:, 0:UH * TILES].rearrange("p (u w) -> p u w", u=UH)
                 for b in range(2)]
        assert 4 * EP == GROUPS * GCOLS
        dst_f = FT[:, EP:2 * EP]
        dst_i = FT[:, 2 * EP:3 * EP].bitcast(I32)
        quot_f = FT[:, 2 * EP:3 * EP]
        quot_i = FT[:, 3 * EP:4 * EP].bitcast(I32)
        rest_f = FT[:, 3 * EP:4 * EP]
        wrong = FT[:, 0:EP]
        ident = sb("ident", [P, P])
        ones = sb("ones", [P, P])
        below = sb("below", [P, P])
        ramp_i = sb("ramp_i", [P, P], I32)
        zero16 = sb("zero16", [P, P], BF16)
        stats = sb("stats", [NP, TILES, 6])
        gstats = [sb(f"gstats{k}", [NP, GT, 6]) for k in range(2)]
        ln_a = sb("ln_a", [NP, TILES])
        ln_b = sb("ln_b", [NP, TILES])
        ln_c = sb("ln_c", [NP, TILES])
        ln_d = sb("ln_d", [NP, TILES])
        rstd = sb("rstd", [NP, TILES])
        shift = sb("shift", [NP, TILES])
        eps = sb("eps", [P, 1])
        hist = sb("hist", [NP, TILES])
        upto = sb("upto", [NP, TILES])
        last_f = sb("last_f", [NP, TILES])
        last_i = sb("last_i", [NP, GT * (GROUPS + GBODY)], I32)
        inv_deg = sb("inv_deg", [NP, TILES])
        empty = sb("empty", [NP, TILES])
        prefix = sb("prefix", [NP, 1])
        first_i = sb("first_i", [P, 1], I32)
        first_f = sb("first_f", [P, 1])
        prev_i = sb("prev_i", [P, 1], I32)
        prev_f = sb("prev_f", [P, 1])
        joins = sb("joins", [P, 1])
        spans = sb("spans", [P, 1])
        chain_end_i = sb("chain_end_i", [P, 1], I32)
        chain_end = sb("chain_end", [P, 1])
        first_last = sb("first_last", [P, 1])
        fix_ok = sb("fix_ok", [P, 1])
        fix_f = sb("fix_f", [P, 1])
        fix_i = sb("fix_i", [P, 1], I32)
        diag = sb("diag", [P, P])
        span_mul = sb("span_mul", [D, P])
        span_add = sb("span_add", [D, P])
        chainT = sb("chainT", [D, P + 1])
        fix_rows = sb("fix_rows", [P, D])
        bstats = sb("bstats", [D, GROUPS, 6])
        bmv = sb("bmv", [D, 2])
        bstd = sb("bstd", [D, 1])
        bscale = sb("bscale", [D, 1])
        bshift = sb("bshift", [D, 1])
        Wl = sb("Wl", [D, D])
        Wr = sb("Wr", [D, D])
        Wmo = [None] + [sb(f"Wmo{k}", [D + 1, 2 * D]) for k in (1, 2)]
        We = [None, sb("We1", [P, 4 * D]), sb("We2", [P, 4 * D])]
        cols = sb("cols", [D, 3])

        psum = ctx.enter_context(nc.psum_tensor("psum", [P, 8 * 512], F32))
        bank = [psum[:, n * 512:(n + 1) * 512] for n in range(8)]
        ramp = bank[5][:, 0:P]
        HIST = bank[7][0:NP, 0:TILES]

        s_xblock = [sem(f"s_xblock{n}") for n in range(5)]
        s_dst = sem("s_dst")
        s_edge = sem("s_edge")
        s_w = sem("s_w")
        s_clear = sem("s_clear")
        s_const = sem("s_const")
        s_v = sem("s_v")
        s_same = sem("s_same")
        s_cen = sem("s_cen")
        s_sq = sem("s_sq")
        s_var = sem("s_var")
        s_std = sem("s_std")
        s_norm = sem("s_norm")
        s_scaled = sem("s_scaled")
        s_h0 = sem("s_h0")
        s_dstf = sem("s_dstf")
        s_quot = sem("s_quot")
        s_tab = [sem(f"s_tab{k}") for k in range(3)]
        s_idx = [[sem(f"s_idx{k}{b}") for b in range(2)] for k in range(3)]
        s_gath = [[sem(f"s_gath{k}{b}") for b in range(2)] for k in range(3)]
        s_wrote = [[sem(f"s_wrote{k}{b}") for b in range(2)] for k in range(3)]
        s_mask = [sem(f"s_mask{k}") for k in range(3)]
        s_chain = [sem(f"s_chain{k}") for k in range(3)]
        s_ea = [None] + [[sem(f"s_ea{k}{b}") for b in range(2)] for k in (1, 2)]
        s_q = [None] + [sem(f"s_q{k}") for k in (1, 2)]
        s_qadd = [None] + [sem(f"s_qadd{k}") for k in (1, 2)]
        s_oh = sem("s_oh")
        s_ohmul = sem("s_ohmul")
        s_hist0 = sem("s_hist0")
        s_hist = sem("s_hist")
        s_upto = sem("s_upto")
        s_prefix = sem("s_prefix")
        s_lastf = sem("s_lastf")
        s_lastd = sem("s_lastd")
        s_flast = sem("s_flast")
        s_fixi = sem("s_fixi")
        s_diag = sem("s_diag")
        s_span = sem("s_span")
        s_go = sem("s_go")
        s_actgo = sem("s_actgo")
        s_dvego = sem("s_dvego")
        s_tail = [sem(f"s_tail{k}") for k in range(3)]
        s_scan = [sem(f"s_scan{k}") for k in range(3)]
        s_back = [sem(f"s_back{k}") for k in range(3)]
        s_fixz = [sem(f"s_fixz{k}") for k in range(3)]
        s_fixg = [sem(f"s_fixg{k}") for k in range(3)]
        s_fixed = [sem(f"s_fixed{k}") for k in range(3)]
        s_fixw = [sem(f"s_fixw{k}") for k in range(3)]
        s_slot = [sem(f"s_slot{k}") for k in range(3)]
        s_ext = [[sem(f"s_ext{k}{s}") for s in range(GBODY)] for k in range(3)]
        s_mean = sem("s_mean")
        s_tA = [sem(f"s_tA{k}") for k in range(3)]
        s_eA = [sem(f"s_eA{k}") for k in range(3)]
        s_src = [sem(f"s_src{k}") for k in range(3)]
        s_tX = [sem(f"s_tX{k}") for k in range(3)]
        s_eX = [sem(f"s_eX{k}") for k in range(3)]
        s_mX = [sem(f"s_mX{k}") for k in range(3)]
        s_fX = [sem(f"s_fX{k}") for k in range(3)]
        s_split = sem("s_split")
        s_mm = sem("s_mm")
        s_ft = sem("s_ft")
        s_bst = sem("s_bst")
        s_bvar = sem("s_bvar")
        s_bstd = sem("s_bstd")
        s_bn = sem("s_bn")
        s_y = sem("s_y")
        s_yT = sem("s_yT")
        s_x1 = sem("s_x1")
        s_x1c = sem("s_x1c")
        s_bnst = sem("s_bnst")
        s_x1b = sem("s_x1b")
        s_h1 = sem("s_h1")
        s_c = sem("s_c")
        s_pm = [None] + [sem(f"s_pm{k}") for k in (1, 2)]
        s_pe = [None] + [sem(f"s_pe{k}") for k in (1, 2)]
        s_keep = sem("s_keep")
        s_c2 = sem("s_c2")
        s_out = sem("s_out")

        STEPS = U + 1
        CHAIN_ALL = STEPS * 2 * CLOOPS + LASTU + 1
        XT = TILES // 5
        TABLE_DONE = [32 * 5] + [32 * (GLOOPS + 1)] * 2
        LASTQ = 2

        def groups(eng, body, ahead=None):
            if ahead:
                ahead(0, 0, 0)
            with eng.Fori(0, GLOOPS) as i:
                for s in range(GBODY):
                    if ahead:
                        ahead(i * GBODY + (s + 1), (s + 1) % GBODY, i + (s + 1) // GBODY)
                    body(i * GBODY + s, s, i)
            body(GROUPS - 1, 0, GLOOPS)

        def pairs(eng, pair, extra=None):
            if extra:
                with eng.Fori(0, GROUPS) as i:
                    pair(i)
                    extra(i)
            with eng.Fori(GROUPS if extra else 0, CLOOPS) as i:
                pair(i)

        def chunks(eng, body, extra=None):
            def pair(i):
                for b in range(2):
                    body(i * 2 + b, i, b, U, i * (2 * U) + b * U)
            pairs(eng, pair, extra)
            body(2 * CLOOPS, CLOOPS, 0, LASTU, LASTCOL)

        def node_dma(eng, to, of, done):
            eng.dma_start(to[0:NWIDE], of[0:NWIDE]).then_inc(done, 16)
            eng.dma_start(to[NWIDE:NP], of[NWIDE:NP]).then_inc(done, 16)

        def group_of(t, g):
            return t[:, bass.ds(g * GT, GT), :]

        def ft_of(g):
            return FT[0:D, bass.ds(g * GCOLS, GCOLS)]

        def wide(b, cols=GCOLS):
            return bank[b][0:D, 0:cols]

        def narrow(b):
            return bank[b][0:NP, 0:GT * D].rearrange("p (t d) -> p t d", t=GT)

        def one_hot_blocks(c, u):
            return [(h, c * 2 + h, h * UH, min(UH, u - h * UH)) for h in range(2) if u > h * UH]

        def squares(n):
            return gbuf[n % 2][0:NP, 0:XT, :]

        def slot(s):
            return gbuf[1][:, s * GT:(s + 1) * GT, :]

        block = ctx.enter_context(nc.Block())

        @block.sync
        def _(sp):
            def load_indices(k, c, i, b, u, col):
                sp.wait_ge(s_gath[k][b], i * (16 * U))
                sp.dma_start(idx[b][:, 0:u], src_v[:, bass.ds(col, u)]).then_inc(s_idx[k][b], 16)

            def load_edges(k, c, i, b, u):
                sp.wait_ge(s_q[k], c * QG)
                if u == U:
                    sp.dma_start(ea_q[b], ea_main[bass.ds(c, 1)].rearrange("a k q p -> (a k) q p")) \
                        .then_inc(s_ea[k][b], 16)
                else:
                    sp.dma_start(ea_q[b][:, 0, :], ea_tail).then_inc(s_ea[k][b], 16)
                    sp.dma_start(ea_q[b][0:DE, 1, :], ea_last).then_inc(s_ea[k][b], 16)

            def store_table(k):
                with sp.Fori(0, GLOOPS) as i:
                    sp.wait_ge(s_pe[k], i * GBODY + GBODY + 2)
                    at = bass.ds(i * (GBODY * GT), GBODY * GT)
                    node_dma(sp, table_v[:, at, :], R[:, at, :], s_tab[k])
                sp.wait_ge(s_pe[k], GROUPS + 2)
                node_dma(sp, table_v[:, TILES - GT:TILES, :], R[:, TILES - GT:TILES, :], s_tab[k])

            for n in range(5):
                at = slice(n * XT, (n + 1) * XT)
                node_dma(sp, X[:, at, :], x_v[:, at, :], s_xblock[n])
            sp.dma_start(dst_i, dst_v).then_inc(s_dst, 16)
            sp.dma_start(first_i[:, :], dst_v[:, 0:1], allow_slow_non_contiguous=True).then_inc(s_edge, 16)
            sp.wait_ge(s_clear, 5)
            sp.dma_start(prev_i[1:P, :], dst_v[0:P - 1, EP - 1:EP],
                         allow_slow_non_contiguous=True).then_inc(s_edge, 16)
            for to, of in ((Wl, wlT), (Wr, wrT)):
                sp.dma_start(to[:, :], of).then_inc(s_w, 16)
            for n, of in enumerate((bl, gamma, beta)):
                sp.dma_start(cols[:, n:n + 1], of.rearrange("(d a) -> d a", a=1)).then_inc(s_w, 16)
            for k, msg, root, bias in ((1, w1_msg, w1_root, b1), (2, w2_msg, w2_root, b2)):
                sp.dma_start(Wmo[k][0:D, 0:D], msg).then_inc(s_w, 16)
                sp.dma_start(Wmo[k][0:D, D:2 * D], root).then_inc(s_w, 16)
                sp.dma_start(Wmo[k][D:D + 1, D:2 * D], bias.rearrange("(a d) -> a d", a=1)).then_inc(s_w, 16)
            for to, of in ((We[1], w1_edge), (We[2], w2_edge)):
                for n in range(4):
                    sp.dma_start(to[n * DE:(n + 1) * DE, n * D:(n + 1) * D], of).then_inc(s_w, 16)
            for n in range(5):
                at = slice(n * XT, (n + 1) * XT)
                sp.wait_ge(s_h0, n + 1)
                node_dma(sp, table_v[:, at, :], R[:, at, :], s_tab[0])
            chunks(sp, lambda c, i, b, u, col: load_indices(0, c, i, b, u, col))
            sp.wait_ge(s_lastf, 1)
            sp.dma_start(last_v, last_f[:, :]).then_inc(s_lastd, 16)
            for k in (1, 2):
                store_table(k)
                for b in range(2):
                    sp.wait_ge(s_gath[k - 1][b], 16 * (U * CLOOPS + (LASTU if b == 0 else 0)))

                def load(c, i, b, u, col, k=k):
                    load_indices(k, c, i, b, u, col)
                    load_edges(k, c, i, b, u)
                chunks(sp, load)
            with sp.Fori(0, GLOOPS) as i:
                sp.wait_ge(s_c2, (i * GBODY + GBODY) * 3)
                at = bass.ds(i * (GBODY * GT), GBODY * GT)
                node_dma(sp, out_v[:, at, :], X[:, at, :], s_out)
            sp.wait_ge(s_c2, GROUPS * 3)
            node_dma(sp, out_v[:, TILES - GT:TILES, :], X[:, TILES - GT:TILES, :], s_out)
            sp.wait_ge(s_out, 32 * (GLOOPS + 1))

        @block.gpsimd
        def _(pool):
            pool.memset(ident[:, :], 0.0).then_inc(s_const, 1)
            pool.memset(ones[:, :], 1.0).then_inc(s_const, 1)
            pool.memset(zero16[:, :], 0.0).then_inc(s_hist0, 1)
            pool.wait_ge(s_const, 2)
            pool.affine_select(out=ident[:, :], in_=ident[:, :], compare_op=ALU.not_equal, fill=1.0,
                               base=0, pattern=[[-1, P]], channel_multiplier=1).then_inc(s_const, 1)
            pool.affine_select(out=below[:, :], in_=ones[:, :], compare_op=ALU.is_gt, fill=0.0,
                               base=0, pattern=[[1, P]], channel_multiplier=-1).then_inc(s_const, 1)
            pool.iota(ramp_i[:, :], pattern=[[1, P]], base=0, channel_multiplier=0).then_inc(s_const, 1)
            pool.iota(chain_end_i[:, :], pattern=[[0, 1]], base=EP - 1, channel_multiplier=EP) \
                .then_inc(s_const, 1)

            for n in range(5):
                at = slice(n * XT, (n + 1) * XT)
                pool.wait_ge(s_norm, n + 1)
                pool.tensor_tensor(R[:, at, :], R[:, at, :], rstd[:, at].unsqueeze(2).to_broadcast([NP, XT, D]),
                                   ALU.mult).then_inc(s_scaled, 1)

            def gather(k, c, i, b, u, col):
                pool.wait_ge(s_idx[k][b], i * 16 + 16)
                pool.wait_ge(s_wrote[k][b], i * 16)
                pool.sem_inc(s_go, 1)
                for n in range(u):
                    pool.indirect_dma_start(
                        out=gbuf[b][:, n, :], out_offset=None, in_=table[:, :],
                        in_offset=bass.IndirectOffsetOnAxis(ap=idx[b][:, n:n + 1], axis=0)) \
                        .then_inc(s_gath[k][b], 16)

            def fetch(k, g, s):
                pool.wait_ge(s_slot[k], g * 2 + 2)
                pool.sem_inc(s_go, 1)
                for t in range(GT):
                    pool.indirect_dma_start(
                        out=slot(s)[:, t, :], out_offset=None, in_=states[:, :],
                        in_offset=bass.IndirectOffsetOnAxis(ap=lidx[s][:, t:t + 1], axis=0),
                        bounds_check=E - 1, oob_is_err=False).then_inc(s_ext[k][s], 16)

            for k in range(3):
                pool.wait_ge(s_tab[k], TABLE_DONE[k])
                if k:
                    pool.wait_ge(s_slot[k - 1], 2 * (GROUPS + GBODY))
                chunks(pool, lambda c, i, b, u, col, k=k: gather(k, c, i, b, u, col))
                if k == 0:
                    pool.wait_ge(s_lastd, 16)
                    pool.wait_ge(s_edge, 32)
                    pool.indirect_dma_start(
                        out=first_last[:, :], out_offset=None, in_=last_dram[:, :],
                        in_offset=bass.IndirectOffsetOnAxis(ap=first_i[:, :], axis=0),
                        bounds_check=N - 1, oob_is_err=False).then_inc(s_flast, 16)
                    pool.wait_ge(s_fixi, 1)
                pool.wait_ge(s_wrote[k][0], 16 * (CLOOPS + 1))
                pool.wait_ge(s_wrote[k][1], 16 * CLOOPS)
                pool.wait_ge(s_fixz[k], 1)
                pool.indirect_dma_start(
                    out=fix_rows[:, :], out_offset=None, in_=states[:, :],
                    in_offset=bass.IndirectOffsetOnAxis(ap=fix_i[:, :], axis=0),
                    bounds_check=E - 1, oob_is_err=False).then_inc(s_fixg[k], 16)
                pool.wait_ge(s_fixed[k], 1)
                pool.indirect_dma_start(
                    out=states[:, :], out_offset=bass.IndirectOffsetOnAxis(ap=fix_i[:, :], axis=0),
                    in_=fix_rows[:, :], in_offset=None,
                    bounds_check=E - 1, oob_is_err=False).then_inc(s_fixw[k], 16)
                pool.wait_ge(s_fixw[k], 16)
                groups(pool, lambda g, s, i, k=k: fetch(k, g, s))

        @block.scalar
        def _(act):
            for n in range(7):
                if n < 5:
                    act.wait_ge(s_cen, n + 1)
                    nc.scalar.activation(squares(n), R[:, n * XT:(n + 1) * XT, :], ACT.Square).then_inc(s_sq, 1)
                if 1 <= n < 6:
                    act.wait_ge(s_var, n)
                    at = slice((n - 1) * XT, n * XT)
                    nc.scalar.activation(ln_a[:, at], ln_b[:, at], ACT.Sqrt, scale=1.0 / D,
                                         bias=eps[0:NP, :]).then_inc(s_std, 1)
                if n >= 2:
                    act.wait_ge(s_scaled, n - 1)
                    at = slice((n - 2) * XT, (n - 1) * XT)
                    nc.scalar.activation(R[:, at, :], R[:, at, :], ACT.Relu).then_inc(s_h0, 1)
                if n == 1:
                    act.wait_ge(s_dst, 16)
                    nc.scalar.copy(dst_f, dst_i).then_inc(s_dstf, 1)
                if n == 3:
                    act.wait_ge(s_dstf, 1)
                    nc.scalar.activation(quot_i, dst_f, ACT.Copy, scale=1.0 / TILES).then_inc(s_quot, 1)
            act.wait_ge(s_quot, 1)
            nc.scalar.copy(quot_f, quot_i).then_inc(s_quot, 1)

            def stage_mask(k, b, u, col):
                if k == 0:
                    nc.scalar.copy(mask[b][:, 0:u], same[:, bass.ds(col, u)]).then_inc(s_mask[k], 1)
                else:
                    nc.scalar.activation(mask[b][:, 0:u], same[:, bass.ds(col, u)], ACT.Copy,
                                         scale=BIG, bias=-BIG).then_inc(s_mask[k], 1)

            def store_states(k, c, b, u, col):
                act.wait_ge(s_chain[k], c * STEPS + u + 1)
                act.dma_start(states_v[:, bass.ds(col, u), :], gbuf[b][:, 0:u, :]).then_inc(s_wrote[k][b], 16)

            def own_term(k, g):
                if k == 1:
                    for t in range(GT):
                        normed_tile(0, g, t, s_src[1])
                else:
                    nc.scalar.copy(nodeA[0][:, :, :], group_of(OWN if k else R, g)).then_inc(s_src[k], 1)
                act.wait_ge(s_tX[k], g + 1)
                nc.scalar.copy(featA[0][0:D, :], wide(6 if k else 2)).then_inc(s_eX[k], 1)
                act.wait_ge(s_mX[k], g + 1)
                act.sem_inc(s_actgo, 1)
                if k:
                    nc.scalar.copy(group_of(OWN, g), narrow(7)).then_inc(s_fX[k], 1)
                else:
                    nc.scalar.activation(ft_of(g), wide(4), ACT.Identity, bias=cols[:, 0:1]).then_inc(s_fX[0], 1)

            def normed_tile(k, g, t, done):
                at = bass.ds(g * GT + t, 1)
                nc.scalar.activation(nodeA[k][:, t, :], X[:, at, :].rearrange("p a d -> p (a d)"), ACT.Relu,
                                     bias=shift[:, at], scale=rstd[:, at]).then_inc(done, 1)

            def states_pass(k):
                def pair(i):
                    for b in range(2):
                        stage_mask(k, b, U, i * (2 * U) + b * U)
                    for b in range(2):
                        store_states(k, i * 2 + b, b, U, i * (2 * U) + b * U)
                pairs(act, pair, lambda g: own_term(k, g))
                stage_mask(k, 0, LASTU, LASTCOL)
                store_states(k, 2 * CLOOPS, 0, LASTU, LASTCOL)

            def copy_products(g, s, i):
                act.wait_ge(s_c, g * 2 + 2)
                nc.scalar.copy(group_of(OWN, g), nodeA[s % 2][:, :, :]).then_inc(s_keep, 1)
                act.wait_ge(s_tA[2], g + 3)
                nc.scalar.copy(featA[s % 2][0:D, :], wide(s % 2)).then_inc(s_eA[2], 1)
                act.wait_ge(s_pm[2], g + 3)
                act.sem_inc(s_actgo, 1)
                nc.scalar.copy(group_of(R, g), narrow(4 + s % 2)).then_inc(s_pe[2], 1)

            act.wait_ge(s_same, 1)
            act.wait_ge(s_w, 16 * N_W)
            act.wait_ge(s_split, 1)
            states_pass(0)

            def copy_means(g, s, i):
                act.wait_ge(s_tA[0], g + 3)
                act.wait_ge(s_mm, g + 1)
                nc.scalar.copy(featA[s % 2][0:D, :], wide(s % 2)).then_inc(s_eA[0], 1)
            groups(act, copy_means)
            act.wait_ge(s_bvar, 1)
            nc.scalar.activation(bstd[:, :], bmv[:, 1:2], ACT.Sqrt, bias=eps[0:D, :]).then_inc(s_bstd, 1)
            act.wait_ge(s_bn, 1)

            def batch_norm(g, s, i):
                act.wait_ge(s_yT, g + 1)
                nc.scalar.activation(featA[s % 2][0:D, :], ft_of(g), ACT.Relu, bias=bshift[:, :],
                                     scale=bscale[:, :]).then_inc(s_y, 1)

            def store_x(g, s, i):
                act.wait_ge(s_x1, g + 3)
                nc.scalar.copy(group_of(X, g), nodeA[s % 2][:, :, :]).then_inc(s_x1c, 1)
            groups(act, store_x, batch_norm)
            act.wait_ge(s_var, 6)
            nc.scalar.activation(ln_a[:, :], ln_b[:, :], ACT.Sqrt, scale=1.0 / D,
                                 bias=eps[0:NP, :]).then_inc(s_std, 1)
            act.wait_ge(s_norm, 6)

            def second_norm(g, s, i):
                act.wait_ge(s_tA[1], g + 1)
                for t in range(GT):
                    normed_tile(s % 2, g, t, s_h1)
            groups(act, second_norm)
            act.wait_ge(s_tA[1], GROUPS + 2)
            act.wait_ge(s_pm[1], GROUPS + 2)
            states_pass(1)
            act.wait_ge(s_tab[1], TABLE_DONE[1])
            groups(act, copy_products)
            states_pass(2)

        @block.tensor
        def _(pe):
            pe.sem_inc(s_ohmul, 2)
            pe.sem_inc(s_tA[0], 2)
            pe.sem_inc(s_tA[1], 2)
            pe.sem_inc(s_tA[2], 2)
            pe.sem_inc(s_yT, 2)
            pe.sem_inc(s_mm, 2)
            pe.sem_inc(s_pm[1], 2)
            pe.sem_inc(s_pm[2], 2)
            pe.sem_inc(s_q[1], QG)
            pe.sem_inc(s_q[2], QG)

            def transpose_nodes(b, tile, done):
                for t in range(GT):
                    last = nc.tensor.transpose(bank[b][0:D, t * NP:(t + 1) * NP], tile(t), ident[0:NP, 0:NP])
                last.then_inc(done, 1)

            def per_node(b, feat, w, done):
                for t in range(GT):
                    last = nc.tensor.matmul(bank[b][0:NP, t * D:(t + 1) * D],
                                            feat[0:w.shape[0], t * NP:(t + 1) * NP], w, start=True, stop=True)
                last.then_inc(done, 1)

            def chain_tails(k):
                pe.wait_ge(s_chain[k], CHAIN_ALL)
                nc.tensor.transpose(bank[6][0:D, 0:P], gbuf[0][:, LASTU - 1, :], ident[:, :]).then_inc(s_tail[k], 1)
                pe.wait_ge(s_scan[k], 1)
                nc.tensor.transpose(bank[7][:, 0:D], chainT[:, 0:P], ident[0:D, 0:D]).then_inc(s_back[k], 1)

            pe.wait_ge(s_hist0, 1)
            nc.tensor.matmul(HIST, zero16[:, 0:NP], zero16[:, 0:TILES], start=True, stop=False,
                             skip_group_check=True)

            def histogram(c, i, b, u, col):
                for h, use, _, count in one_hot_blocks(c, u):
                    pe.wait_ge(s_oh, use * 2 + 2)
                    for n in range(count):
                        last = nc.tensor.matmul(HIST, oh_hi[h][:, n, :], oh_lo[h][:, n, :], start=False,
                                                stop=(u == LASTU and n == u - 1), skip_group_check=True)
                    last.then_inc(s_ohmul if u == U else s_hist, 1)

            def own_term(k, g):
                pe.wait_ge(s_src[k], g * (GT if k == 1 else 1) + (GT if k == 1 else 1))
                transpose_nodes(6 if k else 2, lambda t: nodeA[0][:, t, :], s_tX[k])
                pe.wait_ge(s_eX[k], g + 1)
                if k:
                    per_node(7, featA[0], Wmo[k][:, D:2 * D], s_mX[k])
                else:
                    nc.tensor.matmul(wide(4), Wr[:, :], featA[0][0:D, :], start=True, stop=True) \
                        .then_inc(s_mX[k], 1)

            chunks(pe, histogram, lambda g: own_term(0, g))
            pe.wait_ge(s_const, 6)
            pe.wait_ge(s_upto, 1)
            nc.tensor.matmul(bank[6][0:NP, 0:1], below[0:NP, 0:NP], upto[:, TILES - 1:TILES],
                             start=True, stop=True).then_inc(s_prefix, 1)
            pe.wait_ge(s_diag, 1)
            nc.tensor.matmul(bank[5][0:D, 0:P], ones[:, 0:D], diag[:, :], start=True, stop=True).then_inc(s_span, 1)
            chain_tails(0)
            pe.wait_ge(s_w, 16 * N_W)

            def first_layer(g, s, i):
                pe.wait_ge(s_mean, g + 1)
                pe.wait_ge(s_eA[0], g + 1)
                transpose_nodes(s % 2, lambda t: nodeA[s % 2][:, t, :], s_tA[0])
                pe.wait_ge(s_eA[0], g + 3)
                pe.wait_ge(s_ft, g + 1)
                nc.tensor.matmul(wide(4 + s % 2), Wl[:, :], featA[s % 2][0:D, :], start=True, stop=True) \
                    .then_inc(s_mm, 1)
            groups(pe, first_layer)

            def back_to_nodes(g, s, i):
                pe.wait_ge(s_y, g + 1)
                pe.wait_ge(s_x1, g + 1)
                for t in range(GT):
                    last = nc.tensor.transpose(bank[s % 2][0:NP, t * D:(t + 1) * D],
                                               featA[s % 2][0:D, t * NP:(t + 1) * NP], ident[0:D, 0:D])
                last.then_inc(s_yT, 1)
            groups(pe, back_to_nodes)

            def turn(k, g, s, source, per_group):
                pe.wait_ge(source, g * per_group + per_group)
                pe.wait_ge(s_eA[k], g + 1)
                transpose_nodes(s % 2, lambda t: nodeA[s % 2][:, t, :], s_tA[k])

            def messages(k, g, s):
                pe.wait_ge(s_eA[k], g + 3)
                pe.wait_ge(s_pe[k], g + 1)
                per_node(4 + s % 2, featA[s % 2], Wmo[k][0:D, 0:D], s_pm[k])

            def edge_products(k, c, i, b, u):
                pe.wait_ge(s_ea[k][b], i * 16 + (16 if u == U else 32))
                for q in range(QG if u == U else LASTQ):
                    pe.wait_ge(s_qadd[k], c * QG + (q + 1))
                    if u == U or q == 0:
                        nc.tensor.matmul(bank[q][:, 0:4 * D], ea_q[b][:, q, :], We[k][:, :],
                                         start=True, stop=True).then_inc(s_q[k], 1)
                    else:
                        nc.tensor.matmul(bank[q][:, 0:D], ea_q[b][0:DE, q, :], We[k][0:DE, 0:D],
                                         start=True, stop=True).then_inc(s_q[k], 1)

            def first_conv(g, s, i):
                turn(2, g, s, s_c, 2)
                messages(2, g, s)

            for k in (1, 2):
                if k == 1:
                    groups(pe, lambda g, s, i: messages(1, g, s), lambda g, s, i: turn(1, g, s, s_h1, GT))
                else:
                    groups(pe, first_conv)
                pe.wait_ge(s_pe[k], GROUPS + 2)
                chunks(pe, lambda c, i, b, u, col: edge_products(k, c, i, b, u), lambda g: own_term(k, g))
                chain_tails(k)

        @block.vector
        def _(dve):
            steps = [0]

            def link(ins):
                steps[0] += 1
                ins.then_inc(s_v, 1)
                dve.wait_ge(s_v, steps[0])

            tt, ts, stt = nc.vector.tensor_tensor, nc.vector.tensor_scalar, nc.vector.scalar_tensor_tensor
            copy, memset = nc.vector.tensor_copy, nc.vector.memset
            for ring, size in ((s_eA[0], 2), (s_eA[1], 2), (s_eA[2], 2), (s_x1, 2), (s_pe[1], 2), (s_pe[2], 2),
                               (s_qadd[1], QG), (s_qadd[2], QG), (s_ft, 2), (s_keep, 2), (s_x1c, 2)):
                dve.sem_inc(ring, size)
            memset(We[1][:, :], 0.0).then_inc(s_clear, 1)
            memset(We[2][:, :], 0.0).then_inc(s_clear, 1)
            memset(prev_i[:, :], -1).then_inc(s_clear, 1)
            memset(Wmo[1][D:D + 1, :], 0.0).then_inc(s_clear, 1)
            memset(Wmo[2][D:D + 1, :], 0.0).then_inc(s_clear, 1)
            for k in range(2):
                link(memset(featA[k][D:D + 1, :], 1.0))
            link(memset(eps[:, :], EPS))

            def variance(at):
                w = [stats[:, at, f:f + 1].rearrange("p t a -> p (t a)") for f in range(6)]
                a, b, c, d = (t[:, at] for t in (ln_d, ln_b, ln_c, shift))
                link(tt(a, w[1], w[4], ALU.subtract))
                link(tt(c, w[1], w[4], ALU.add))
                link(tt(d, w[2], w[5], ALU.add))
                link(tt(b, a, a, ALU.mult))
                stt(out=b, in0=b, scalar=D / 4.0, in1=d, op0=ALU.mult, op1=ALU.add).then_inc(s_var, 1)

            def scale_and_shift(at, n):
                dve.wait_ge(s_std, n)
                link(nc.vector.reciprocal(rstd[:, at], ln_a[:, at]))
                stt(out=shift[:, at], in0=ln_c[:, at], scalar=-0.5, in1=rstd[:, at], op0=ALU.mult,
                    op1=ALU.mult).then_inc(s_norm, 1)

            def centre(n):
                at = slice(n * XT, (n + 1) * XT)
                dve.wait_ge(s_xblock[n], 32)
                link(nc.vector.reduce_sum(ln_c[:, at], X[:, at, :], axis=mybir.AxisListType.X))
                link(ts(ln_c[:, at], ln_c[:, at], -1.0 / D, None, ALU.mult))
                tt(R[:, at, :], X[:, at, :], ln_c[:, at].unsqueeze(2).to_broadcast([NP, XT, D]), ALU.add) \
                    .then_inc(s_cen, 1)

            centre(0)
            for n in range(5):
                if n < 4:
                    centre(n + 1)
                at = slice(n * XT, (n + 1) * XT)
                dve.wait_ge(s_sq, n + 1)
                nc.vector.reduce_sum(ln_b[:, at], squares(n), axis=mybir.AxisListType.X).then_inc(s_var, 1)
                dve.wait_ge(s_std, n + 1)
                nc.vector.reciprocal(rstd[:, at], ln_a[:, at]).then_inc(s_norm, 1)

            dve.wait_ge(s_dstf, 1)
            link(memset(same[:, 0:1], 0.0))
            tt(same[:, 1:EP], dst_f[:, 1:EP], dst_f[:, 0:EP - 1], ALU.is_equal).then_inc(s_same, 1)
            dve.wait_ge(s_quot, 2)
            link(stt(out=rest_f, in0=quot_f, scalar=-float(TILES), in1=dst_f, op0=ALU.mult, op1=ALU.add))
            for test, bound, up in ((ALU.is_ge, float(TILES), 1.0), (ALU.is_lt, 0.0, -1.0)):
                link(ts(wrong, rest_f, bound, None, test))
                link(stt(out=quot_f, in0=wrong, scalar=up, in1=quot_f, op0=ALU.mult, op1=ALU.add))
                link(stt(out=rest_f, in0=wrong, scalar=-up * TILES, in1=rest_f, op0=ALU.mult, op1=ALU.add))
            link(copy(hi[:, :], quot_f))
            link(copy(lo[:, :], rest_f))
            dve.wait_ge(s_edge, 32)
            dve.wait_ge(s_const, 6)
            link(copy(first_f[:, :], first_i[:, :]))
            link(copy(prev_f[:, :], prev_i[:, :]))
            link(copy(chain_end[:, :], chain_end_i[:, :]))
            link(tt(joins[:, :], first_f[:, :], prev_f[:, :], ALU.is_equal))
            link(tt(spans[:, :], first_f[:, :], dst_f[:, EP - 1:EP], ALU.is_equal))
            link(tt(spans[:, :], spans[:, :], joins[:, :], ALU.mult))
            ts(diag[:, :], ident[:, :], spans[:, 0:1], None, ALU.mult).then_inc(s_diag, 1)
            link(copy(ramp, ramp_i[:, :]))
            link(memset(first_last[:, :], NOWHERE))
            link(memset(last_i[:, :], 0))
            for s in range(GBODY):
                link(memset(lidx[s][:, :], int(NOWHERE)))
            link(memset(chainT[:, 0:1], 0.0))
            dve.sem_inc(s_split, 1)

            def last_edges():
                dve.wait_ge(s_hist, 1)
                link(copy(hist[:, :], HIST))
                link(nc.vector.tensor_tensor_scan(out=upto[:, :], data0=ones[0:NP, 0:TILES], data1=hist[:, :],
                                                  initial=0.0, op0=ALU.mult, op1=ALU.add))
                dve.sem_inc(s_upto, 1)
                link(ts(empty[:, :], hist[:, :], 0.0, None, ALU.is_equal))
                link(ts(hist[:, :], hist[:, :], 1.0, None, ALU.max))
                link(nc.vector.reciprocal(inv_deg[:, :], hist[:, :]))
                dve.wait_ge(s_prefix, 1)
                link(copy(prefix[:, :], bank[6][0:NP, 0:1]))
                link(ts(last_f[:, :], upto[:, :], prefix[:, 0:1], -1.0, ALU.add, ALU.add))
                stt(out=last_f[:, :], in0=empty[:, :], scalar=NOWHERE, in1=last_f[:, :], op0=ALU.mult,
                    op1=ALU.add).then_inc(s_lastf, 1)
                dve.wait_ge(s_lastf, 1)
                link(copy(last_i[:, 0:TILES], last_f[:, :]))
                dve.wait_ge(s_span, 1)
                link(copy(span_mul[:, :], bank[5][0:D, 0:P]))
                link(ts(span_add[:, :], span_mul[:, :], -1.0, BIG, ALU.add, ALU.mult))

            def chain(k, c, i, b, u, col):
                if k == 0:
                    for h, use, at, count in one_hot_blocks(c, u):
                        dve.wait_ge(s_ohmul, use + 1)
                        for to, of, w in ((oh_hi[h], hi, NP), (oh_lo[h], lo, TILES)):
                            tt(to[:, 0:count, :], ramp[:, 0:w].unsqueeze(1).to_broadcast([P, count, w]),
                               of[:, bass.ds(col + at, count)].unsqueeze(2).to_broadcast([P, count, w]),
                               ALU.is_equal).then_inc(s_oh, 1)
                    if u == LASTU:
                        last_edges()
                dve.wait_ge(s_gath[k][b], i * (16 * U) + 16 * u)
                if k:
                    for q in range(QG if u == U else LASTQ):
                        dve.wait_ge(s_q[k], c * QG + (q + 1 + QG))
                        n = min(4, u - 4 * q)
                        rows = gbuf[b][:, 4 * q:4 * q + n, :].rearrange("p n d -> p (n d)")
                        tt(rows, rows, bank[q][:, 0:n * D], ALU.add).then_inc(s_qadd[k], 1)
                dve.wait_ge(s_mask[k], c + 1)
                ops = (ALU.mult, ALU.add) if k == 0 else (ALU.add, ALU.max)
                before = carry[:, :]
                for n in range(u):
                    if k and n % 4 == 0:
                        dve.wait_ge(s_qadd[k], c * QG + (n // 4 + 1 + QG))
                    dve.wait_ge(s_chain[k], c * STEPS + n)
                    row = gbuf[b][:, n, :]
                    stt(out=row, in0=before, scalar=mask[b][:, n:n + 1], in1=row, op0=ops[0], op1=ops[1]) \
                        .then_inc(s_chain[k], 1)
                    before = row
                dve.wait_ge(s_chain[k], c * STEPS + u)
                copy(carry[:, :], before).then_inc(s_chain[k], 1)

            def complete_segments(k):
                memset(fix_rows[:, :], 0.0).then_inc(s_fixz[k], 1)
                if k == 0:
                    dve.wait_ge(s_flast, 16)
                    link(tt(fix_ok[:, :], first_last[:, :], chain_end[:, :], ALU.is_le))
                    link(tt(fix_ok[:, :], fix_ok[:, :], joins[:, :], ALU.mult))
                    link(ts(fix_f[:, :], first_last[:, :], -NOWHERE, fix_ok[:, 0:1], ALU.add, ALU.mult))
                    ts(fix_i[:, :], fix_f[:, :], NOWHERE, None, ALU.add).then_inc(s_fixi, 1)
                dve.wait_ge(s_tail[k], 1)
                nc.vector.tensor_tensor_scan(
                    out=chainT[:, 1:P + 1], data0=(span_add if k else span_mul)[:, :],
                    data1=bank[6][0:D, 0:P], initial=0.0, op0=ALU.add if k else ALU.mult,
                    op1=ALU.max if k else ALU.add).then_inc(s_scan[k], 1)
                for s in range(GBODY):
                    if s == 0:
                        dve.wait_ge(s_wrote[k][1], 16 * CLOOPS)
                    prepare(k, s, s)
                dve.wait_ge(s_fixg[k], 16)
                dve.wait_ge(s_back[k], 1)
                tt(fix_rows[:, :], fix_rows[:, :], bank[7][:, 0:D], ALU.max if k else ALU.add) \
                    .then_inc(s_fixed[k], 1)

            def prepare(k, g, s):
                memset(slot(s), 0.0).then_inc(s_slot[k], 1)
                copy(lidx[s][0:NP, :], last_i[:, bass.ds(g * GT, GT)]).then_inc(s_slot[k], 1)

            def fetched(k, s, i):
                dve.wait_ge(s_ext[k][s], i * (16 * GT) + 16 * GT)

            link(memset(carry[:, :], 0.0))
            chunks(dve, lambda c, i, b, u, col: chain(0, c, i, b, u, col))
            complete_segments(0)

            dve.wait_ge(s_fX[0], GROUPS)

            def means(g, s, i):
                fetched(0, s, i)
                dve.wait_ge(s_tA[0], g + 1)
                tt(nodeA[s % 2][:, :, :], slot(s)[0:NP],
                   inv_deg[:, bass.ds(g * GT, GT)].unsqueeze(2).to_broadcast([NP, GT, D]), ALU.mult) \
                    .then_inc(s_mean, 1)
                dve.wait_ge(s_mean, g + 1)
                prepare(0, g + GBODY, s)

            def add_neighbours(g, s, i):
                dve.wait_ge(s_mm, g + 3)
                tt(ft_of(g), ft_of(g), wide(4 + s % 2), ALU.add).then_inc(s_ft, 1)
                dve.wait_ge(s_ft, g + 3)
                nc.vector.bn_stats(bstats[:, bass.ds(g, 1), :].rearrange("p a f -> p (a f)"), ft_of(g)) \
                    .then_inc(s_bst, 1)
            groups(dve, add_neighbours, means)
            dve.wait_ge(s_bst, GROUPS)
            nc.vector.bn_aggr(bmv[:, :], bstats[:, :, :].rearrange("p g f -> p (g f)")).then_inc(s_bvar, 1)
            dve.wait_ge(s_bstd, 1)
            dve.wait_ge(s_w, 16 * N_W)
            link(nc.vector.reciprocal(bstd[:, :], bstd[:, :]))
            link(tt(bscale[:, :], bstd[:, :], cols[:, 1:2], ALU.mult))
            link(tt(bshift[:, :], bmv[:, 0:1], bscale[:, :], ALU.mult))
            tt(bshift[:, :], cols[:, 2:3], bshift[:, :], ALU.subtract).then_inc(s_bn, 1)

            def add_first_layer(g, s, i):
                dve.wait_ge(s_yT, g + 3)
                dve.wait_ge(s_x1c, g + 1)
                dve.sem_inc(s_dvego, 1)
                tt(nodeA[s % 2][:, :, :], group_of(X, g), narrow(s % 2), ALU.add).then_inc(s_x1, 1)
                dve.wait_ge(s_x1, g + 3)
                for t in range(GT):
                    nc.vector.bn_stats(gstats[s % 2][:, t, :], nodeA[s % 2][:, t, :]).then_inc(s_bnst, 1)
                dve.wait_ge(s_bnst, g * GT + GT)
                copy(stats[:, bass.ds(g * GT, GT), :], gstats[s % 2][:, :, :]).then_inc(s_x1b, 1)
            groups(dve, add_first_layer)
            dve.wait_ge(s_x1b, GROUPS)
            variance(slice(0, TILES))
            scale_and_shift(slice(0, TILES), 6)

            def copy_transposed(g, s, i):
                dve.wait_ge(s_tA[1], g + 3)
                dve.wait_ge(s_pm[1], g + 1)
                copy(featA[s % 2][0:D, :], wide(s % 2)).then_inc(s_eA[1], 1)

            def copy_messages(g, s, i):
                dve.wait_ge(s_pm[1], g + 3)
                copy(group_of(R, g), narrow(4 + s % 2)).then_inc(s_pe[1], 1)
            dve.wait_ge(s_tab[0], TABLE_DONE[0])
            groups(dve, copy_messages, copy_transposed)

            def max_pass(k):
                link(memset(carry[:, :], 0.0))
                chunks(dve, lambda c, i, b, u, col: chain(k, c, i, b, u, col))
                dve.wait_ge(s_fX[k], GROUPS)
                complete_segments(k)

            max_pass(1)

            def first_conv(g, s, i):
                fetched(1, s, i)
                dve.wait_ge(s_tA[2], g + 1)
                dve.wait_ge(s_keep, g + 1)
                tt(nodeA[s % 2][:, :, :], slot(s)[0:NP], group_of(OWN, g), ALU.add).then_inc(s_c, 1)
                dve.wait_ge(s_c, g * 2 + 1)
                stt(out=nodeA[s % 2][:, :, :], in0=nodeA[s % 2][:, :, :], scalar=SLOPE,
                    in1=nodeA[s % 2][:, :, :], op0=ALU.mult, op1=ALU.max).then_inc(s_c, 1)
                prepare(1, g + GBODY, s)
            groups(dve, first_conv)
            max_pass(2)

            def second_conv(g, s, i):
                fetched(2, s, i)
                tt(nodeA[s % 2][:, :, :], slot(s)[0:NP], group_of(OWN, g), ALU.add).then_inc(s_c2, 1)
                dve.wait_ge(s_c2, g * 3 + 1)
                stt(out=nodeA[s % 2][:, :, :], in0=nodeA[s % 2][:, :, :], scalar=SLOPE,
                    in1=nodeA[s % 2][:, :, :], op0=ALU.mult, op1=ALU.max).then_inc(s_c2, 1)
                dve.wait_ge(s_c2, g * 3 + 2)
                tt(group_of(X, g), group_of(X, g), nodeA[s % 2][:, :, :], ALU.add).then_inc(s_c2, 1)
                prepare(2, g + GBODY, s)
            groups(dve, second_conv)


def kernel(**inputs):
    import numpy as np
    import concourse.bacc as bacc
    from concourse.bass_utils import run_bass_kernel_spmd

    nc = bacc.Bacc("TRN2", target_bir_lowering=False, num_devices=1)
    given = {k: np.asarray(v) for k, v in inputs.items()}
    ea = given["edge_attr_32"].reshape(P, EP, DE)
    main = ea[:, :LASTCOL].reshape(P, 2 * CLOOPS, QG, 4, DE).transpose(1, 3, 4, 2, 0)
    tail = ea[:, LASTCOL:LASTCOL + 4].reshape(P, 4 * DE).transpose(1, 0)
    arrays = {
        "x": given["x"], "src": given["src"], "dst": given["dst"],
        "ea_main": main.reshape(2 * CLOOPS, 4 * DE, QG, P), "ea_tail": tail,
        "ea_last": ea[:, EP - 1].transpose(1, 0),
        "wlT": given["L0_gnn_Wl"].T, "bl": given["L0_gnn_bl"], "wrT": given["L0_gnn_Wr"].T,
        "gamma": given["L0_gnn_gamma"], "beta": given["L0_gnn_beta"],
    }
    for layer in "12":
        for name, key in (("msg", "W{}_msg"), ("edge", "W{}_edge"), ("root", "W{}_root")):
            arrays[f"w{layer}_{name}"] = given["L1_gnn_" + key.format(layer)]
        arrays[f"b{layer}"] = given[f"L1_gnn_b{layer}"]
    arrays = {f"in_{k}": np.ascontiguousarray(v) for k, v in arrays.items()}
    args = {k[3:]: nc.dram_tensor(k, a.shape, mybir.dt.from_np(a.dtype), kind="ExternalInput").ap()
            for k, a in arrays.items()}
    out = nc.dram_tensor("out_0", (N, D), F32, kind="ExternalOutput").ap()
    gnn_kernel(nc, out=out, **args)
    r = run_bass_kernel_spmd(nc, [arrays], core_ids=[0])
    return r.results[0]["out_0"]
```
